# Optimizing a Trainium2 kernel written in Bass

```python
import numpy as np
import jax
import jax.numpy as jnp

def _softmax(x, axis=-1):
    return jax.nn.softmax(x, axis=axis)

def _gelu(x):
    return jax.nn.gelu(x, approximate=True)

def _silu(x):
    return jax.nn.silu(x)

def _sigmoid(x):
    return jax.nn.sigmoid(x)

def _layernorm(x, axis=-1, eps=1e-05):
    m = jnp.mean(x, axis=axis, keepdims=True)
    v = jnp.var(x, axis=axis, keepdims=True)
    return (x - m) / jnp.sqrt(v + eps)

def _scatter_add(tgt, idx, src, axis=0):
    return tgt.at[idx].add(src)

def _segment_sum(src, seg, n):
    return jax.ops.segment_sum(src, seg, n)
kernel_name = 'mk_adaln_d1_jaxref_r4_2ac7ad'

def setup_inputs(seed: int=0):
    np.random.seed(seed)
    _w = jnp.asarray

    def _L0_attn_setup():
        import jax, jax.numpy as jnp
        import numpy as np
        HEAD = 64

        def wkv6(r, k, v, w, u):
            B, T, C = r.shape
            N = C // HEAD
            shp = lambda a: a.reshape(B, T, N, HEAD).transpose(1, 0, 2, 3)
            rT, kT, vT = (shp(r), shp(k), shp(v))
            dT = jnp.exp(shp(w))
            uu = u[None]

            def step(S, inp):
                rt, kt, vt, dt = inp
                kv = vt[..., :, None] * kt[..., None, :]
                yt = jnp.einsum('bnj,bnij->bni', rt, S + uu[..., None, :] * kv)
                S = S * dt[..., None, :] + kv
                return (S, yt)
            S0 = jnp.zeros((B, N, HEAD, HEAD), r.dtype)
            _, ys = jax.lax.scan(step, S0, (rT, kT, vT, dT))
            return ys.transpose(1, 0, 2, 3).reshape(B, T, C)
        key = jax.random.key(seed)
        B, T, C = (2, 256, 256)
        N = C // HEAD
        depth, layer_id = (24, 12)
        r01 = layer_id / (depth - 1)
        r1a0 = 1.0 - layer_id / depth
        ddd = np.arange(C, dtype=np.float64) / C
        miu_x = (1.0 - ddd ** (0.6 * r1a0 ** 0.9)).reshape(1, 1, C).astype(np.float32)
        lam = np.stack([1.0 - ddd ** (0.9 * r1a0), 1.0 - ddd ** (0.9 * r1a0) - 0.4 * r01, 1.0 - ddd ** (0.4 * r1a0) - 0.6 * r01, 1.0 - ddd ** (0.2 * r1a0), 1.0 - ddd ** (0.2 * r1a0)]).reshape(5, 1, 1, C).astype(np.float32)
        n = np.arange(C, dtype=np.float64)
        td_miu = (-6.0 + 5.5 * (n / (C - 1)) ** (0.85 + 1.0 * r01 ** 0.5)).reshape(1, 1, C).astype(np.float32)
        zigzag = ((n + 1) % 3 - 1) * 0.1
        u = (r01 * (2.5 - n / (C - 1)) + zigzag).reshape(N, HEAD).astype(np.float32)
        ks = jax.random.split(key, 12)
        unif = lambda k, shape, s: jax.random.uniform(k, shape, jnp.float32, -s, s)
        x = jax.random.normal(ks[0], (B, T, C), jnp.float32)
        return {'x': x, 'miu_x': jnp.asarray(miu_x), 'lam': jnp.asarray(lam), 'A': unif(ks[1], (C, 160), 0.01), 'Bp': unif(ks[2], (5, 32, C), 0.01), 'td_miu': jnp.asarray(td_miu), 'tdA': unif(ks[3], (C, 64), 0.01), 'tdB': unif(ks[4], (64, C), 0.01), 'u': jnp.asarray(u), 'Wk': unif(ks[5], (C, C), 0.05 / C ** 0.5), 'Wv': unif(ks[6], (C, C), 0.5 / C ** 0.5), 'Wr': unif(ks[7], (C, C), 0.5 / C ** 0.5), 'Wo': unif(ks[8], (C, C), 0.5 / C ** 0.5), 'Wg1': unif(ks[9], (C, 160), 0.01), 'Wg2': unif(ks[10], (160, C), 0.01), 'gamma': jnp.ones((C,), jnp.float32), 'beta': jnp.zeros((C,), jnp.float32)}
    _L0_attn_in = _L0_attn_setup()

    def _L0_ffn_setup():
        import jax, jax.numpy as jnp
        import numpy as np
        import math
        B, L, D = (4, 1024, 256)
        F = 1024
        E = 16
        CAP_FACTOR = 1.0
        EPS = 1e-05
        key = jax.random.key(seed)
        ks = jax.random.split(key, 8)
        std = 0.02
        return {'x': jax.random.normal(ks[0], (B, L, D), dtype=jnp.float32), 'norm_weight': jnp.ones((D,), dtype=jnp.float32), 'router_weight': jax.random.normal(ks[1], (E, D), dtype=jnp.float32) * std, 'router_bias': jnp.zeros((E,), dtype=jnp.float32), 'fc1_weight': jax.random.normal(ks[2], (E, F, D), dtype=jnp.float32) * std, 'fc1_bias': jnp.zeros((E, F), dtype=jnp.float32), 'fc2_weight': jax.random.normal(ks[3], (E, D, F), dtype=jnp.float32) * std, 'fc2_bias': jnp.zeros((E, D), dtype=jnp.float32)}
    _L0_ffn_in = _L0_ffn_setup()
    _L0_c = _w((lambda *s: np.random.randn(*s).astype(np.float32) * 0.05)(32, 256))
    _L0_wmod = _w((lambda *s: np.random.randn(*s).astype(np.float32) * 0.05)(256, 6 * 256) * 256 ** (-0.5))
    _d = {'L0_attn_x': _L0_attn_in['x'], 'L0_attn_miu_x': _L0_attn_in['miu_x'], 'L0_attn_lam': _L0_attn_in['lam'], 'L0_attn_A': _L0_attn_in['A'], 'L0_attn_Bp': _L0_attn_in['Bp'], 'L0_attn_td_miu': _L0_attn_in['td_miu'], 'L0_attn_tdA': _L0_attn_in['tdA'], 'L0_attn_tdB': _L0_attn_in['tdB'], 'L0_attn_u': _L0_attn_in['u'], 'L0_attn_Wk': _L0_attn_in['Wk'], 'L0_attn_Wv': _L0_attn_in['Wv'], 'L0_attn_Wr': _L0_attn_in['Wr'], 'L0_attn_Wo': _L0_attn_in['Wo'], 'L0_attn_Wg1': _L0_attn_in['Wg1'], 'L0_attn_Wg2': _L0_attn_in['Wg2'], 'L0_attn_gamma': _L0_attn_in['gamma'], 'L0_attn_beta': _L0_attn_in['beta'], 'L0_ffn_norm_weight': _L0_ffn_in['norm_weight'], 'L0_ffn_router_weight': _L0_ffn_in['router_weight'], 'L0_ffn_router_bias': _L0_ffn_in['router_bias'], 'L0_ffn_fc1_weight': _L0_ffn_in['fc1_weight'], 'L0_ffn_fc1_bias': _L0_ffn_in['fc1_bias'], 'L0_ffn_fc2_weight': _L0_ffn_in['fc2_weight'], 'L0_ffn_fc2_bias': _L0_ffn_in['fc2_bias'], 'L0_c': _L0_c, 'L0_wmod': _L0_wmod}
    _x0 = _d['L0_attn_x']
    _d['L0_attn_x'] = jax.random.normal(jax.random.fold_in(jax.random.key(seed), 1), (32, 512, 256), dtype=_x0.dtype)
    del _x0
    return _d

def reference(L0_attn_x, L0_attn_miu_x, L0_attn_lam, L0_attn_A, L0_attn_Bp, L0_attn_td_miu, L0_attn_tdA, L0_attn_tdB, L0_attn_u, L0_attn_Wk, L0_attn_Wv, L0_attn_Wr, L0_attn_Wo, L0_attn_Wg1, L0_attn_Wg2, L0_attn_gamma, L0_attn_beta, L0_ffn_norm_weight, L0_ffn_router_weight, L0_ffn_router_bias, L0_ffn_fc1_weight, L0_ffn_fc1_bias, L0_ffn_fc2_weight, L0_ffn_fc2_bias, L0_c, L0_wmod):

    def _L0_attn_ref(x, miu_x, lam, A, Bp, td_miu, tdA, tdB, u, Wk, Wv, Wr, Wo, Wg1, Wg2, gamma, beta):
        import jax, jax.numpy as jnp
        import numpy as np
        HEAD = 64

        def wkv6(r, k, v, w, u):
            B, T, C = r.shape
            N = C // HEAD
            shp = lambda a: a.reshape(B, T, N, HEAD).transpose(1, 0, 2, 3)
            rT, kT, vT = (shp(r), shp(k), shp(v))
            dT = jnp.exp(shp(w))
            uu = u[None]

            def step(S, inp):
                rt, kt, vt, dt = inp
                kv = vt[..., :, None] * kt[..., None, :]
                yt = jnp.einsum('bnj,bnij->bni', rt, S + uu[..., None, :] * kv)
                S = S * dt[..., None, :] + kv
                return (S, yt)
            S0 = jnp.zeros((B, N, HEAD, HEAD), r.dtype)
            _, ys = jax.lax.scan(step, S0, (rT, kT, vT, dT))
            return ys.transpose(1, 0, 2, 3).reshape(B, T, C)
        B, T, C = x.shape
        N = C // HEAD
        x_last = jnp.concatenate([jnp.zeros_like(x[:, :1]), x[:, :-1]], axis=1)
        b_a = x_last - x
        xx = x + b_a * miu_x
        h = jnp.tanh(xx @ A).reshape(5, B * T, 32)
        miu = jnp.einsum('smk,skc->smc', h, Bp).reshape(5, B, T, C) + lam
        x5 = x[None] + b_a[None] * miu
        w_in, k_in, v_in, r_in, g_in = (x5[0], x5[1], x5[2], x5[3], x5[4])
        w = td_miu + jnp.tanh(w_in @ tdA) @ tdB
        k = k_in @ Wk.T * jnp.exp(jnp.minimum(w, 0.0))
        v = v_in @ Wv.T
        r = r_in @ Wr.T
        g = jnp.tanh(g_in @ Wg1) @ Wg2
        y = wkv6(r, k, v, w, u)
        yh = y.reshape(B, T, N, HEAD)
        mean = yh.mean(-1, keepdims=True)
        var = yh.var(-1, keepdims=True)
        yn = (yh - mean) / jnp.sqrt(var + 1e-05 * N)
        yn = yn.reshape(B, T, C) * gamma + beta
        return yn * g @ Wo.T

    def _L0_ffn_ref(x, norm_weight, router_weight, router_bias, fc1_weight, fc1_bias, fc2_weight, fc2_bias):
        import jax, jax.numpy as jnp
        import numpy as np
        import math
        B, L, D = (4, 1024, 256)
        F = 1024
        E = 16
        CAP_FACTOR = 1.0
        EPS = 1e-05
        b, l, d = x.shape
        n_tokens = b * l
        n_experts = router_weight.shape[0]
        capacity = max(1, math.ceil(CAP_FACTOR * n_tokens / n_experts))
        top_k = min(capacity, n_tokens)
        xf = x.reshape(n_tokens, d)
        rms = jnp.sqrt(jnp.mean(xf * xf, axis=-1, keepdims=True) + EPS)
        xn = xf / rms * norm_weight
        logits = xn @ router_weight.T + router_bias
        probs = jax.nn.softmax(logits, axis=-1)
        _, idx = jax.lax.top_k(logits.T, top_k)
        xe = xn[idx]
        h = jnp.einsum('ecd,efd->ecf', xe, fc1_weight) + fc1_bias[:, None, :]
        h = jax.nn.gelu(h, approximate=False)
        y = jnp.einsum('ecf,edf->ecd', h, fc2_weight) + fc2_bias[:, None, :]
        gates = jnp.take_along_axis(probs.T, idx, axis=1)
        flat_idx = idx.reshape(-1)
        contrib = (y * gates[:, :, None]).reshape(-1, d)
        output = jnp.zeros((n_tokens, d), dtype=x.dtype).at[flat_idx].add(contrib)
        gate_sums = jnp.zeros((n_tokens, 1), dtype=x.dtype).at[flat_idx].add(gates.reshape(-1, 1))
        assigned = gate_sums > 0
        output = jnp.where(assigned, output / jnp.where(assigned, gate_sums, 1.0), output)
        return output.reshape(b, l, d)
    x = L0_attn_x
    mod = (_silu(L0_c) @ L0_wmod).reshape(L0_c.shape[0], 6, 1, -1)
    sa, ca, ga, sb, cb, gb = (mod[:, 0], mod[:, 1], mod[:, 2], mod[:, 3], mod[:, 4], mod[:, 5])
    ga = (2 * (ga >= 0) - 1) * jnp.maximum(jnp.abs(ga), 0.25)
    gb = (2 * (gb >= 0) - 1) * jnp.maximum(jnp.abs(gb), 0.25)
    h = _layernorm(x, axis=-1) * (1 + ca) + sa
    x = x + ga * _L0_attn_ref(h, L0_attn_miu_x, L0_attn_lam, L0_attn_A, L0_attn_Bp, L0_attn_td_miu, L0_attn_tdA, L0_attn_tdB, L0_attn_u, L0_attn_Wk, L0_attn_Wv, L0_attn_Wr, L0_attn_Wo, L0_attn_Wg1, L0_attn_Wg2, L0_attn_gamma, L0_attn_beta)
    h = _layernorm(x, axis=-1) * (1 + cb) + sb
    x = x + gb * _L0_ffn_ref(h, L0_ffn_norm_weight, L0_ffn_router_weight, L0_ffn_router_bias, L0_ffn_fc1_weight, L0_ffn_fc1_bias, L0_ffn_fc2_weight, L0_ffn_fc2_bias)
    return x

_drawn_inputs = setup_inputs


def setup_inputs(seed=0):
    import zlib

    import numpy as np

    out = dict(_drawn_inputs(seed))
    spreads = {'L0_attn_gamma': (1.0, 0.6),
     'L0_attn_beta': (0.0, 0.8),
     'L0_ffn_norm_weight': (1.0, 0.6),
     'L0_ffn_router_bias': (0.0, 2.0),
     'L0_ffn_fc1_bias': (0.0, 0.8),
     'L0_ffn_fc2_bias': (0.0, 0.45)}
    factors = {'L0_attn_miu_x': 8.0,
     'L0_attn_lam': 8.0,
     'L0_attn_A': 8.0,
     'L0_attn_Bp': 8.0,
     'L0_attn_td_miu': 8.0,
     'L0_attn_tdA': 8.0,
     'L0_attn_tdB': 8.0,
     'L0_attn_u': 8.0,
     'L0_attn_Wk': 8.0,
     'L0_attn_Wv': 8.0,
     'L0_attn_Wr': 8.0,
     'L0_attn_Wo': 8.0,
     'L0_attn_Wg1': 8.0,
     'L0_attn_Wg2': 8.0,
     'L0_ffn_fc1_weight': 2.813}
    for name, (base, spread) in spreads.items():
        noise = np.random.default_rng([zlib.crc32(name.encode()), seed]).standard_normal(out[name].shape)
        drawn = base * np.exp(spread * noise) if base else spread * noise
        out[name] = jnp.asarray(drawn.astype(out[name].dtype))
    for name, factor in factors.items():
        out[name] = (out[name] * factor).astype(out[name].dtype)
    return out
```

```python
from contextlib import ExitStack

import numpy as np

import concourse.bass as bass
from concourse import mybir

F32 = mybir.dt.float32
I32 = mybir.dt.int32
F32R = mybir.dt.float32r
ALU = mybir.AluOpType
ACT = mybir.ActivationFunctionType
AX = mybir.AxisListType

P = 128
C = 256
CT = C // P
T = 512
NC = T // P
H = 4
HD = C // H
NS = 5
LR = 32
WR = 64
GR = 160
E = 16
F = 1024
FT = F // P
TW = C + E
AW = C + 1
LN_EPS = 1e-5
GN_EPS = 1e-5 * H
RMS_EPS = 1e-5

MIUX, LAM, TDMIU, BONUS, GAMMA, BETA, NCOL = 0, 1, 6, 7, 8, 9, 10
GA, CB, SB, GB = range(4)


class Signal:

    def __init__(self, sem, per=1, unit=1):
        self.sem, self.per, self.unit = sem, per, unit


class Row:

    def __init__(self, n, half, odd):
        self.n, self.half, self.odd = n, half, odd


def need(eng, signal, row, k=None, back=0):
    value = (signal.per * (row.n - back) + (signal.per if k is None else k)) * signal.unit
    if isinstance(value, int) and value <= 0:
        return
    eng.wait_ge(signal.sem, value)


def settle(eng, keep):
    eng.sem_inc(keep["passed"], 1)


def need_dma(eng, signals, row, back=0):
    signal = signals[row.odd]
    value = (row.half + 1 - back // 2) * signal.per * 16
    if isinstance(value, int) and value <= 0:
        return
    eng.wait_ge(signal.sem, value)


def pipeline(eng, total, lags, step):
    most = max(lags)
    head = min(most + 2 + most % 2, total)
    last = total - (total - head) % 2

    def peeled(t):
        rows = [Row(t - g, (t - g) // 2, (t - g) % 2) if 0 <= t - g < total else None for g in lags]
        step(*rows)

    for t in range(head):
        peeled(t)
    if last > head:
        with eng.Fori(head // 2, last // 2) as turn:
            for u in range(2):
                rows = []
                for g in lags:
                    half = turn + (u - g) // 2
                    rows.append(Row(turn * 2 + (u - g), half, (u - g) % 2))
                step(*rows)
    for t in range(last, total + most):
        peeled(t)


def high_part(nc, out, src):
    return nc.vector.tensor_copy(out.bitcast(F32R), src)


def low_part(eng, out, src, high):
    return eng.tensor_tensor(out.bitcast(F32R), src, high, ALU.subtract)


class Banks:

    def __init__(self, ctx, nc, first, count, jobs, tag):
        self.tiles = [ctx.enter_context(nc.psum_tensor(f"{tag}{k}", [P, 512], F32)) for k in range(count)]
        per = [(len(jobs) - k + count - 1) // count for k in range(count)]
        self.filled = [Signal(ctx.enter_context(nc.semaphore(f"{tag}{k}_filled")), per[k]) for k in range(count)]
        self.drained = [Signal(ctx.enter_context(nc.semaphore(f"{tag}{k}_drained")), per[k]) for k in range(count)]
        self.at = {job: (n % count, n // count) for n, job in enumerate(jobs)}

    def tile(self, job):
        return self.tiles[self.at[job][0]]

    def wait_free(self, eng, row, job):
        bank, turn = self.at[job]
        need(eng, self.drained[bank], row, turn)

    def wait_filled(self, eng, row, job, back=0):
        bank, turn = self.at[job]
        need(eng, self.filled[bank], row, turn + 1, back)

    def wait_drained(self, eng, row, job, back=0):
        bank, turn = self.at[job]
        need(eng, self.drained[bank], row, turn + 1, back)

    def fill(self, ins, job):
        ins.then_inc(self.filled[self.at[job][0]].sem, 1)

    def drain(self, ins, job):
        ins.then_inc(self.drained[self.at[job][0]].sem, 1)


def setup(nc, ins, dram, keep, NB):
    with ExitStack() as ctx:
        def sb(name, shape, dt=F32):
            return ctx.enter_context(nc.sbuf_tensor(name, shape, dt))

        def sem(name):
            return ctx.enter_context(nc.semaphore(name))

        wmod = sb("wmod", [P, CT, 6 * C])
        cT = sb("cT", [P, CT, NB])
        sig = sb("sig", [P, CT, NB])
        silu = sb("silu", [P, CT, NB])
        row_sb = sb("row_sb", [NB, 6 * C])
        sign = sb("sign", [NB, C])
        mag = sb("mag", [NB, C])
        rows = sb("rows", [NB, 4, C])
        s_of = sb("s_of", [P, 32], I32)
        t_of = sb("t_of", [P, 32], I32)
        xor = sb("xor", [P, 32], I32)
        later = sb("later", [P, 32], I32)
        ge = sb("ge", [P, 32], I32)
        pad = sb("pad", [P, C])
        psR = [ctx.enter_context(nc.psum_tensor(f"psR{k}", [P, 512], F32)) for k in range(3)]
        psC = ctx.enter_context(nc.psum_tensor("psC", [P, 512], F32))

        loaded, made, e_done = sem("setup_loaded"), sem("setup_made"), sem("setup_exp")
        silu_done, mod_done, stored, chain = sem("silu_done"), sem("mod_done"), sem("mod_stored"), sem("setup_chain")
        block = ctx.enter_context(nc.Block())

        @block.sync
        def _(sp):
            sp.dma_start(cT[:, :, :], ins["cT"].rearrange("(c p) b -> p c b", p=P)).then_inc(loaded, 16)
            sp.dma_start(wmod[:, :, :], ins["wmod"].rearrange("(c p) n -> p c n", p=P)).then_inc(loaded, 16)
            sp.dma_start(keep["col"][:, :, :], ins["col"]).then_inc(loaded, 16)
            sp.wait_ge(mod_done, 2)
            sp.dma_start(dram["mod"], rows[:, :, :]).then_inc(stored, 16)
            sp.wait_ge(stored, 16)

        @block.gpsimd
        def _(pool):
            pool.memset(keep["ident"][:, :], 0.0).then_inc(made, 1)
            pool.iota(s_of[:, :], [[0, 32]], base=0, channel_multiplier=1).then_inc(made, 1)
            pool.iota(t_of[:, :], [[1, 32]], base=0, channel_multiplier=0).then_inc(made, 1)
            pool.wait_ge(made, 1)
            pool.affine_select(out=keep["ident"][:, :], in_=keep["ident"][:, :], compare_op=ALU.not_equal, fill=1.0,
                               base=0, pattern=[[-1, P]], channel_multiplier=1).then_inc(made, 1)

        @block.scalar
        def _(act):
            act.wait_ge(loaded, 48)
            nc.scalar.activation(sig[:, :, :], cT[:, :, :], ACT.Exp, scale=-1.0).then_inc(e_done, 1)

        @block.vector
        def _(dve):
            links = [0]

            def link(ins_):
                links[0] += 1
                ins_.then_inc(chain, 1)
                dve.wait_ge(chain, links[0])

            dve.wait_ge(loaded, 48)
            dve.wait_ge(e_done, 1)
            link(nc.vector.tensor_scalar_add(sig[:, :, :], sig[:, :, :], 1.0))
            link(nc.vector.reciprocal(sig[:, :, :], sig[:, :, :]))
            nc.vector.tensor_tensor(silu[:, :, :], cT[:, :, :], sig[:, :, :], ALU.mult).then_inc(silu_done, 1)
            dve.wait_ge(made, 4)
            link(nc.vector.tensor_scalar(s_of[:, :], s_of[:, :], 31, None, ALU.bitwise_and))
            link(nc.vector.tensor_tensor(xor[:, :], s_of[:, :], t_of[:, :], ALU.bitwise_xor))
            link(nc.vector.tensor_tensor(later[:, :], t_of[:, :], s_of[:, :], ALU.is_gt))
            link(nc.vector.tensor_scalar(keep["mask"][:, 0, :], xor[:, :], 0, None, ALU.is_equal))
            for n, half in enumerate((1, 2, 4, 8, 16)):
                link(nc.vector.tensor_scalar(ge[:, :], xor[:, :], half, None, ALU.is_ge))
                link(nc.vector.tensor_tensor(ge[:, :], ge[:, :], later[:, :], ALU.mult))
                link(nc.vector.scalar_tensor_tensor(out=keep["mask"][:, n + 1, :], in0=xor[:, :], scalar=2 * half,
                                                    in1=ge[:, :], op0=ALU.is_lt, op1=ALU.mult))
            dve.wait_ge(mod_done, 1)
            for k in range(3):
                link(nc.vector.tensor_copy(row_sb[:, k * 512:(k + 1) * 512], psR[k][0:NB, :]))
            link(nc.vector.tensor_copy(keep["modT"][:, 0:2, :], psC[:, 0:2 * NB].rearrange("p (k b) -> p k b", k=2)))
            link(nc.vector.tensor_scalar_add(keep["modT"][:, 2:4, :],
                                             psC[:, 2 * NB:4 * NB].rearrange("p (k b) -> p k b", k=2), 1.0))
            for dst, src in ((GA, 2), (GB, 5)):
                v = row_sb[:, src * C:(src + 1) * C]
                link(nc.vector.tensor_scalar(sign[:, :], v, 0.0, 2.0, ALU.is_ge, ALU.mult))
                link(nc.vector.scalar_tensor_tensor(out=mag[:, :], in0=v, scalar=-1.0, in1=v, op0=ALU.mult, op1=ALU.max))
                link(nc.vector.tensor_scalar_max(mag[:, :], mag[:, :], 0.25))
                link(nc.vector.scalar_tensor_tensor(out=rows[:, dst, :], in0=sign[:, :], scalar=-1.0, in1=mag[:, :],
                                                    op0=ALU.add, op1=ALU.mult))
            link(nc.vector.tensor_copy(rows[:, SB, :], row_sb[:, 3 * C:4 * C]))
            nc.vector.tensor_scalar_add(rows[:, CB, :], row_sb[:, 4 * C:5 * C], 1.0).then_inc(mod_done, 1)

        @block.tensor
        def _(pe):
            pe.wait_ge(silu_done, 1)
            for k in range(3):
                for c in range(CT):
                    nc.tensor.matmul(psR[k][0:NB, :], silu[:, c, :], wmod[:, c, k * 512:(k + 1) * 512],
                                     start=(c == 0), stop=(c == CT - 1))
            for k in range(4):
                for c in range(CT):
                    last = nc.tensor.matmul(psC[:, k * NB:(k + 1) * NB], wmod[:, c, k * P:(k + 1) * P],
                                            silu[:, c, :], start=(c == 0), stop=(c == CT - 1))
            last.then_inc(mod_done, 1)


def lora(nc, ins, dram, keep, NB):
    with ExitStack() as ctx:
        def sb(name, shape, dt=F32):
            return ctx.enter_context(nc.sbuf_tensor(name, shape, dt))

        def sig(name, per=1):
            return Signal(ctx.enter_context(nc.semaphore(name)), per)

        ident, modT, col = keep["ident"], keep["modT"], keep["col"]
        A = sb("A", [P, CT, NS * LR])
        half = sb("half", [P, NC])
        x = sb("x", [P, 2, NC, C])
        stats = sb("stats", [P, NC, 6])
        mv = sb("mv", [P, NC, 2])
        var = sb("var", [P, NC])
        rstd = sb("rstd", [P, NC])
        shift = sb("shift", [P, NC])
        xn = sb("xn", [P, NC, C])
        hp = sb("hp", [P, 2, CT, T + 1])
        ba = sb("ba", [P, CT, T])
        xx = sb("xx", [P, 2, CT, T])
        th = sb("th", [P, 2, NC, NS * LR])
        blank = sb("blank", [P, NC, AW])
        jobs = ["xT0", "xT1", "h0", "h1"]
        pb = Banks(ctx, nc, 0, 4, jobs, "lo")

        ready, w_in, blanked = sig("lo_const"), sig("lo_weights"), sig("lo_blanked")
        x_in = [sig(f"lo_x_in{k}") for k in range(2)]
        h_out = [sig(f"lo_h_out{k}", 1) for k in range(2)]
        t_out = [sig(f"lo_t_out{k}", 1) for k in range(2)]
        stat_done, mv_done, var_done = sig("lo_stats"), sig("lo_mean"), sig("lo_var")
        rstd_done, shift_done, xn_done = sig("lo_rstd"), sig("lo_shift"), sig("lo_xn")
        ba_done, xx_done = sig("lo_ba"), sig("lo_xx")
        block = ctx.enter_context(nc.Block())
        lags = (0, 1, 2, 3)

        @block.sync
        def _(sp):
            sp.dma_start(A[:, :, :], ins["A"].rearrange("(c p) n -> p c n", p=P)).then_inc(w_in.sem, 16)
            sp.wait_ge(ready.sem, 1)

            def step(nxt, cur, old, tail):
                if nxt:
                    sp.dma_start(dram["acc"].rearrange("(b c p) d -> b p c d", c=NC, p=P)[nxt.n], blank[:, :, :])\
                      .then_inc(blanked.sem, 16)
                    need(sp, xn_done, nxt, back=2)
                    sp.dma_start(x[:, nxt.odd, :, :], ins["x"][nxt.n].rearrange("(c p) d -> p c d", p=P))\
                      .then_inc(x_in[nxt.odd].sem, 16)
                if old:
                    pb.wait_drained(sp, old, "xT1")
                    sp.dma_start(dram["hT"][old.n].rearrange("(c p) t -> p c t", p=P), hp[:, old.odd, :, 1:T + 1])\
                      .then_inc(h_out[old.odd].sem, 16)
                if tail:
                    pb.wait_drained(sp, tail, "h1")
                    sp.dma_start(dram["lora"][tail.n].rearrange("(c p) k -> p c k", p=P), th[:, tail.odd, :, :])\
                      .then_inc(t_out[tail.odd].sem, 16)

            pipeline(sp, NB, lags, step)
            sp.wait_ge(blanked.sem, 16 * NB)
            for k in range(2):
                sp.wait_ge(h_out[k].sem, 16 * (NB // 2))
                sp.wait_ge(t_out[k].sem, 16 * (NB // 2))

        @block.vector
        def _(dve):
            nc.vector.memset(hp[:, :, :, 0:1], 0.0)
            nc.vector.memset(blank[:, :, :], 0.0)
            nc.vector.memset(half[:, :], -0.5).then_inc(ready.sem, 1)

            def step(nxt, cur, old, tail):
                if cur:
                    need_dma(dve, x_in, cur)
                    for c in range(NC):
                        last = nc.vector.bn_stats(stats[:, c, :], x[:, cur.odd, c, :])
                    last.then_inc(stat_done.sem, 1)
                    need(dve, stat_done, cur)
                    settle(dve, keep)
                    for c in range(NC):
                        last = nc.vector.bn_aggr(mv[:, c, :], stats[:, c, :])
                    last.then_inc(mv_done.sem, 1)
                    need(dve, mv_done, cur)
                    nc.vector.tensor_scalar_add(var[:, :], mv[:, :, 1], LN_EPS).then_inc(var_done.sem, 1)
                if cur:
                    need(dve, rstd_done, cur)
                    need(dve, xn_done, cur, back=1)
                    nc.vector.scalar_tensor_tensor(out=shift[:, :], in0=mv[:, :, 0], scalar=-1.0, in1=rstd[:, :],
                                                   op0=ALU.mult, op1=ALU.mult).then_inc(shift_done.sem, 1)
                if old:
                    need(dve, ba_done, old)
                    pb.wait_filled(dve, old, "h1", back=2)
                    for c in range(CT):
                        last = nc.vector.scalar_tensor_tensor(
                            out=xx[:, old.odd, c, :], in0=ba[:, c, :], scalar=col[:, MIUX, c:c + 1],
                            in1=hp[:, old.odd, c, 1:T + 1], op0=ALU.mult, op1=ALU.add)
                    last.then_inc(xx_done.sem, 1)

            pipeline(dve, NB, lags, step)

        @block.gpsimd
        def _(pool):
            def step(nxt, cur, old, tail):
                if cur:
                    need(pool, var_done, cur)
                    need(pool, xn_done, cur, back=1)
                    if isinstance(cur.n, int) and cur.n == 0:
                        pool.wait_ge(ready.sem, 1)
                    nc.gpsimd.tensor_tensor(rstd[:, :], var[:, :], half[:, :], ALU.pow).then_inc(rstd_done.sem, 1)
                if old:
                    pb.wait_drained(pool, old, "xT1")
                    need(pool, xx_done, old, back=1)
                    for c in range(CT):
                        last = nc.gpsimd.tensor_tensor(ba[:, c, :], hp[:, old.odd, c, 0:T],
                                                       hp[:, old.odd, c, 1:T + 1], ALU.subtract)
                    last.then_inc(ba_done.sem, 1)

            pipeline(pool, NB, lags, step)

        @block.scalar
        def _(act):
            def step(nxt, cur, old, tail):
                if tail:
                    need_dma(act, t_out, tail, back=2)
                    for j in range(2):
                        pb.wait_filled(act, tail, f"h{j}")
                        pb.drain(nc.scalar.activation(
                            th[:, tail.odd, 2 * j:2 * j + 2, :],
                            pb.tile(f"h{j}")[:, 0:2 * NS * LR].rearrange("p (c k) -> p c k", c=2), ACT.Tanh), f"h{j}")
                if cur:
                    need_dma(act, x_in, cur)
                    need(act, shift_done, cur)
                    pb.wait_filled(act, cur, "xT1", back=1)
                    for c in range(NC):
                        last = nc.scalar.activation(xn[:, c, :], x[:, cur.odd, c, :], ACT.Identity,
                                                    bias=shift[:, c:c + 1], scale=rstd[:, c:c + 1])
                    last.then_inc(xn_done.sem, 1)
                    for c in range(CT):
                        pb.wait_filled(act, cur, f"xT{c}")
                        if c == 0:
                            need_dma(act, h_out, cur, back=2)
                            need(act, xx_done, cur, back=2)
                        pb.drain(nc.scalar.activation(hp[:, cur.odd, c, 1:T + 1], pb.tile(f"xT{c}")[:, :], ACT.Identity,
                                                      bias=modT[:, c, bass.ds(cur.n, 1)],
                                                      scale=modT[:, 2 + c, bass.ds(cur.n, 1)]), f"xT{c}")

            pipeline(act, NB, lags, step)

        @block.tensor
        def _(pe):
            pe.wait_ge(w_in.sem, 16)

            def step(nxt, cur, old, tail):
                if tail:
                    need(pe, xx_done, tail)
                    for j in range(2):
                        pb.wait_free(pe, tail, f"h{j}")
                        for q in (2 * j, 2 * j + 1):
                            for c in range(CT):
                                last = nc.tensor.matmul(pb.tile(f"h{j}")[:, (q % 2) * NS * LR:(q % 2 + 1) * NS * LR],
                                                        xx[:, tail.odd, c, q * P:(q + 1) * P], A[:, c, :],
                                                        start=(c == 0), stop=(c == CT - 1))
                        pb.fill(last, f"h{j}")
                if cur:
                    need(pe, xn_done, cur)
                    for c in range(CT):
                        pb.wait_free(pe, cur, f"xT{c}")
                        for q in range(NC):
                            last = nc.tensor.transpose(pb.tile(f"xT{c}")[:, q * P:(q + 1) * P],
                                                       xn[:, q, c * P:(c + 1) * P], ident[:, :])
                        pb.fill(last, f"xT{c}")

            pipeline(pe, NB, lags, step)


S_W, S_K, S_V, S_R, S_G = range(NS)
LEVELS = (1, 2, 4, 8, 16)
T_RING = 5
X5_SLOT = (0, 1, 2, 0, 1)


def mixer(nc, ins, dram, keep, NB):
    with ExitStack() as ctx:
        def sb(name, shape, dt=F32):
            return ctx.enter_context(nc.sbuf_tensor(name, shape, dt))

        def sig(name, per=1, unit=1):
            return Signal(ctx.enter_context(nc.semaphore(name)), per, unit)

        ident, col, mask = keep["ident"], keep["col"], keep["mask"]
        BpP = sb("BpP", [P, 4, C])
        Bp4 = sb("Bp4", [LR, C])
        tdA = sb("tdA", [P, CT, WR])
        tdB = sb("tdB", [WR, C])
        Wk = sb("Wk", [P, CT, C])
        Wv = sb("Wv", [P, CT, C])
        Wr = sb("Wr", [P, CT, C])
        Wo = sb("Wo", [P, CT, C])
        Wg1 = sb("Wg1", [P, CT, GR])
        Wg2 = sb("Wg2", [P, C])
        Wg2b = sb("Wg2b", [GR - P, C])
        Rw = sb("Rw", [P, CT, E])
        nw = sb("nw", [P, C])
        rb = sb("rb", [P, E])
        sel = sb("sel", [P, CT, H])
        HL = 32 + H
        selT = sb("selT", [HL, CT, P])
        half = sb("halfm", [P, NC])
        eps4 = sb("eps4", [H, 1])
        wsum = sb("wsum", [P, CT * H])
        hp = sb("hpm", [P, 2, CT, T + 1])
        Hs = sb("Hs", [P, 2, NS, 4 * LR])
        Hr = sb("Hr", [P, 4, NS, LR])
        hs = sb("hs", [P, T])
        hs4 = sb("hs4", [LR, T])
        ba = sb("bam", [P, CT, T])
        tt = sb("tt", [P, T_RING, T])
        x5 = sb("x5", [P, 3, CT, T])
        tw = sb("tw", [WR, T])
        d = sb("d", [P, 2, CT, T])
        KG = sb("KG", [P, 2, CT, T])
        RF = sb("RF", [P, 3, CT, T])
        v = sb("v", [P, 2, NC, C])
        tg = sb("tg", [P, 2, T])
        tgb = sb("tgb", [GR - P, 2, T])
        full = {L: sb(f"full{L}", [P, CT, T // L]) for L in (2, 4, 8, 16, 32, 64, 128)}
        acc = sb("accm", [P, NC * H, 32])
        AT = sb("AT", [P, NC * H, P])
        KGt = sb("KGt", [P, CT, 3 * P])
        S = sb("S", [P, 3, CT, HD])
        gT = sb("gT", [P, 2, CT, T])
        ys = sb("ys", [P, CT, T])
        ysq = sb("ysq", [P, CT, T])
        std = sb("std", [HL, T])
        rs = sb("rs", [HL, T])
        gn = sb("gn", [P, CT, T])
        WoG = sb("WoG", [P, CT, C])
        x = sb("xm_in", [P, 2, NC, C])
        mb = sb("mb", [P, 2, 3, C])
        xm = sb("xm", [P, NC, C])
        stats = sb("stats2", [P, NC, 6])
        mv = sb("mv2", [P, NC, 2])
        var = sb("var2", [P, NC])
        rstd = sb("rstd2", [P, NC])
        xh = sb("xh", [P, NC, C])
        h2 = sb("h2", [P, NC, C])
        ms = sb("ms", [P, NC])
        msr = sb("msr", [P, NC])
        rr = sb("rr", [P, NC])
        tbl = sb("tbl", [P, 2, NC, TW])
        xnT = sb("xnT", [P, CT, T])
        lgt = sb("lgt", [P, NC, E])
        lmx = sb("lmx", [P, NC])
        lsh = sb("lsh", [P, NC, E])
        lex = sb("lex", [P, NC, E])
        lsum = sb("lsum", [P, NC])
        lrc = sb("lrc", [P, NC])

        pj = Banks(ctx, nc, 0, 3, ["Ht0", "Ht1", "miu00", "miu01", "miu10", "miu11", "tdA", "miu20", "miu21",
                                   "tdB0", "tdB1", "K0", "K1", "miu30", "miu31", "V0", "V1", "miu40", "miu41",
                                   "R0", "R1", "G1a", "G1b"], "pj")
        lv = Banks(ctx, nc, 3, 3, [f"{job}{o}" for job in ("lv1_", "lv2_", "lv4_", "lv8_", "lv16_", "r32_", "G2", "r64_",
                                                           "KT") for o in range(2)] + ["KV", "Y0", "Y1"], "lv")
        tl = Banks(ctx, nc, 6, 2, ["SS", "RB0", "RB1", "WO0", "WO1", "XT0", "XT1", "LG"], "tl")

        zeroed, w_in, const_ok, const_chain = sig("mx_zeroed"), sig("mx_weights"), sig("mx_const"), sig("mx_chain")
        h_in = [sig(f"mx_h_in{k}") for k in range(2)]
        H_in = [sig(f"mx_H_in{k}") for k in range(2)]
        x_in = [sig(f"mx_x_in{k}", 2) for k in range(2)]
        tbl_out = [sig(f"mx_tbl_out{k}") for k in range(2)]
        xm_out = sig("mx_xm_out", 1, 16)
        Hr_done, ba_done, x5_done = sig("Hr_done"), sig("ba_done"), sig("x5_done", 10)
        ru_done, bonus_in, acc_zero, upd_done, acc_copied = sig("ru_done"), sig("bonus_in", 2), sig("acc_zero"), sig("upd_done", 7), sig("acc_copied")
        s_step, rs_step, rs_done, gn_done, wog_done = sig("s_step", 2), sig("rs_step", 2), sig("rs_done"), sig("gn_done", 2), sig("wog_done")
        st_done, mv_done, var_done, rstd_done = sig("st2_done"), sig("mv2_done"), sig("var2_done"), sig("rstd2_done")
        xh_done, h2a_done, h2_done, ms_done = sig("xh_done"), sig("h2a_done"), sig("h2_done"), sig("ms_done")
        msr_done, rr_done, tok_done = sig("msr_done"), sig("rr_done"), sig("tok_done")
        soft, exp_done, kept = sig("soft_step", 5), sig("exp_done"), sig("logits_kept")
        block = ctx.enter_context(nc.Block())
        lags = (0, 1, 2, 3)

        @block.sync
        def _(sp):
            loads = [(tdA[:, :, :], ins["tdA"].rearrange("(c p) n -> p c n", p=P)), (tdB[:, :], ins["tdB"]),
                     (Wk[:, :, :], ins["WkT"].rearrange("(c p) n -> p c n", p=P)),
                     (Wv[:, :, :], ins["WvT"].rearrange("(c p) n -> p c n", p=P)),
                     (Wr[:, :, :], ins["WrT"].rearrange("(c p) n -> p c n", p=P)),
                     (Wo[:, :, :], ins["WoT"].rearrange("(c p) n -> p c n", p=P)),
                     (Wg1[:, :, :], ins["Wg1"].rearrange("(c p) n -> p c n", p=P)),
                     (Wg2[:, :], ins["Wg2"][0:P, :]), (Wg2b[:, :], ins["Wg2"][P:GR, :]),
                     (Rw[:, :, :], ins["RwT"].rearrange("(c p) n -> p c n", p=P)),
                     (nw[:, :], ins["nw"].to_broadcast([P, C])), (rb[:, :], ins["rb"].to_broadcast([P, E])),
                     (sel[:, :, :], ins["sel"]), (Bp4[:, :], ins["Bp"][4])]
            for dst, src in loads:
                sp.dma_start(dst, src).then_inc(w_in.sem, 16)
            sp.wait_ge(zeroed.sem, 1)
            for at in (0, 32):
                sp.dma_start(std[at:at + H, 0:C], ins["selT"].rearrange("h c p -> h (c p)")).then_inc(w_in.sem, 16)
            for s in range(4):
                sp.dma_start(BpP[s * LR:(s + 1) * LR, s, :], ins["Bp"][s]).then_inc(w_in.sem, 16)

            def step(nxt, cur, mid, old):
                if nxt:
                    need(sp, x5_done, nxt, back=2)
                    sp.dma_start(hp[:, nxt.odd, :, 1:T + 1], dram["hT"][nxt.n].rearrange("(c p) t -> p c t", p=P))\
                      .then_inc(h_in[nxt.odd].sem, 16)
                    need(sp, Hr_done, nxt, back=2)
                    flat = dram["lora"].rearrange("b t k -> (b t k)").rearrange("(s b p k) -> b p s k", s=NS, b=NB, p=P)
                    sp.dma_start(Hs[:, nxt.odd, :, :], flat[nxt.n]).then_inc(H_in[nxt.odd].sem, 16)
                if mid:
                    tl.wait_drained(sp, mid, "WO1", back=2)
                    sp.dma_start(x[:, mid.odd, :, :], ins["x"][mid.n].rearrange("(c p) d -> p c d", p=P))\
                      .then_inc(x_in[mid.odd].sem, 16)
                    need(sp, h2_done, mid, back=2)
                    sp.dma_start(mb[:, mid.odd, :, :], dram["mod"][mid.n, 0:3, :].unsqueeze(0).to_broadcast([P, 3, C]))\
                      .then_inc(x_in[mid.odd].sem, 16)
                if old:
                    tl.wait_drained(sp, old, "WO1")
                    sp.dma_start(dram["xmid"][old.n].rearrange("(c p) d -> p c d", p=P), xm[:, :, :])\
                      .then_inc(xm_out.sem, 16)
                    need(sp, soft, old)
                    sp.dma_start(dram["table"].rearrange("(b c p) d -> b p c d", c=NC, p=P)[old.n], tbl[:, old.odd, :, :])\
                      .then_inc(tbl_out[old.odd].sem, 16)

            pipeline(sp, NB, lags, step)
            sp.wait_ge(xm_out.sem, 16 * NB)
            for k in range(2):
                sp.wait_ge(tbl_out[k].sem, 16 * (NB // 2))

        n_weights = 20

        @block.tensor
        def _(pe):
            pe.wait_ge(w_in.sem, 16 * n_weights)
            pe.wait_ge(const_ok.sem, 1)

            def miu(row, s):
                if s == 0:
                    pj.wait_drained(pe, row, "Ht1")
                for c in range(CT):
                    pj.wait_free(pe, row, f"miu{s}{c}")
                    o = pj.tile(f"miu{s}{c}")[:, :]
                    if s < 4:
                        last = nc.tensor.matmul(o, BpP[:, s, c * P:(c + 1) * P], hs[:, :], start=True, stop=True)
                    else:
                        last = nc.tensor.matmul(o, Bp4[:, c * P:(c + 1) * P], hs4[:, :], start=True, stop=True)
                    pj.fill(last, f"miu{s}{c}")

            def project(row, job, w, s, lo, hi):
                pj.wait_free(pe, row, job)
                for c in range(CT):
                    last = nc.tensor.matmul(pj.tile(job)[0:hi - lo, :], w[:, c, lo:hi], x5[:, X5_SLOT[s], c, :],
                                            start=(c == 0), stop=(c == CT - 1))
                pj.fill(last, job)

            def diagonal(row, job, bonus=False):
                wide = 64 if bonus else 32
                for o in range(2):
                    rows = slice(HD * o, HD * o + HD)
                    lv.wait_free(pe, row, f"{job}{o}")
                    settle(pe, keep)
                    for ch in range(NC):
                        for c in range(CT):
                            for q in range(4):
                                t0, at = ch * P + 32 * q, (ch * CT + c) * wide
                                R = RF[rows, row.odd, c, t0:t0 + 32]
                                if bonus:
                                    R = RF[rows, row.odd:3:2 - row.odd, c, t0:t0 + 32]
                                last = nc.tensor.matmul(lv.tile(f"{job}{o}")[32 * q:32 * q + 32, at:at + wide],
                                                        KG[rows, row.odd, c, t0:t0 + 32], R, start=True, stop=True)
                    lv.fill(last, f"{job}{o}")

            def step(nxt, cur, mid, old):
                if mid:
                    pj.wait_drained(pe, mid, "K1")
                    pj.wait_drained(pe, mid, "R1")
                    need(pe, ru_done, mid)
                    diagonal(mid, "lv1_", bonus=True)
                if cur:
                    need(pe, Hr_done, cur)
                    pj.wait_free(pe, cur, "Ht0")
                    for i in range(4):
                        last = nc.tensor.transpose(pj.tile("Ht0")[:, i * P:(i + 1) * P],
                                                   Hr[:, i, 0:4, :].rearrange("p s k -> p (s k)"), ident[:, :])
                    pj.fill(last, "Ht0")
                    pj.wait_free(pe, cur, "Ht1")
                    for i in range(4):
                        last = nc.tensor.transpose(pj.tile("Ht1")[0:LR, i * P:(i + 1) * P],
                                                   Hr[:, i, 4, :], ident[:, :])
                    pj.fill(last, "Ht1")
                if old:
                    lv.wait_drained(pe, old, "Y1")
                    tl.wait_free(pe, old, "SS")
                    for c in range(CT):
                        last = nc.tensor.matmul(tl.tile("SS")[0:H, :], sel[:, c, :], ysq[:, c, :],
                                                start=(c == 0), stop=(c == CT - 1))
                    tl.fill(last, "SS")
                if cur:
                    miu(cur, S_W)
                if mid:
                    need(pe, upd_done, mid, 1)
                    diagonal(mid, "lv2_")
                if cur:
                    miu(cur, S_K)
                if mid:
                    need(pe, upd_done, mid, 2)
                    diagonal(mid, "lv4_")
                if cur:
                    need(pe, x5_done, cur, 2)
                    project(cur, "tdA", tdA, S_W, 0, WR)
                    miu(cur, S_V)
                if old:
                    need(pe, rs_done, old)
                    for c in range(CT):
                        tl.wait_free(pe, old, f"RB{c}")
                        tl.fill(nc.tensor.matmul(tl.tile(f"RB{c}")[:, :], selT[:, c, :].bitcast(F32R), rs[:, :].bitcast(F32R),
                                                 start=True, stop=True), f"RB{c}")
                if mid:
                    need(pe, upd_done, mid, 3)
                    diagonal(mid, "lv8_")
                if cur:
                    pj.wait_drained(pe, cur, "tdA")
                    for c in range(CT):
                        pj.wait_free(pe, cur, f"tdB{c}")
                        pj.fill(nc.tensor.matmul(pj.tile(f"tdB{c}")[:, :], tdB[:, c * P:(c + 1) * P], tw[:, :],
                                                 start=True, stop=True), f"tdB{c}")
                    need(pe, x5_done, cur, 4)
                    for c in range(CT):
                        project(cur, f"K{c}", Wk, S_K, c * P, (c + 1) * P)
                    miu(cur, S_R)
                if old:
                    need(pe, gn_done, old)
                    need(pe, wog_done, old)
                    for j in range(2):
                        tl.wait_free(pe, old, f"WO{j}")
                        for q in (2 * j, 2 * j + 1):
                            for c in range(CT):
                                last = nc.tensor.matmul(tl.tile(f"WO{j}")[:, (q % 2) * C:(q % 2 + 1) * C],
                                                        gn[:, c, q * P:(q + 1) * P], WoG[:, c, :],
                                                        start=(c == 0), stop=(c == CT - 1))
                        tl.fill(last, f"WO{j}")
                if mid:
                    need(pe, upd_done, mid, 4)
                    diagonal(mid, "lv16_")
                if cur:
                    need(pe, x5_done, cur, 6)
                    for j in range(2):
                        pj.wait_free(pe, cur, f"V{j}")
                        for q in (2 * j, 2 * j + 1):
                            for c in range(CT):
                                last = nc.tensor.matmul(pj.tile(f"V{j}")[:, (q % 2) * C:(q % 2 + 1) * C],
                                                        x5[:, X5_SLOT[S_V], c, q * P:(q + 1) * P], Wv[:, c, :],
                                                        start=(c == 0), stop=(c == CT - 1))
                        pj.fill(last, f"V{j}")
                if mid:
                    need(pe, upd_done, mid, 5)
                    for o in range(2):
                        rows = slice(HD * o, HD * o + HD)
                        lv.wait_free(pe, mid, f"r32_{o}")
                        settle(pe, keep)
                        for ch in range(NC):
                            for c in range(CT):
                                for pr in range(2):
                                    t0, at = ch * P + 64 * pr, (ch * CT + c) * 32
                                    last = nc.tensor.matmul(lv.tile(f"r32_{o}")[64 * pr:64 * pr + 32, at:at + 32],
                                                            KG[rows, mid.odd, c, t0:t0 + 32],
                                                            RF[rows, mid.odd, c, t0 + 32:t0 + 64], start=True, stop=True)
                        lv.fill(last, f"r32_{o}")
                    pj.wait_drained(pe, mid, "G1b")
                    for c in range(CT):
                        lv.wait_free(pe, mid, f"G2{c}")
                        nc.tensor.matmul(lv.tile(f"G2{c}")[:, :], Wg2[:, c * P:(c + 1) * P], tg[:, mid.odd, :],
                                         start=True, stop=False)
                        lv.fill(nc.tensor.matmul(lv.tile(f"G2{c}")[:, :], Wg2b[:, c * P:(c + 1) * P],
                                                 tgb[:, mid.odd, :], start=False, stop=True), f"G2{c}")
                if cur:
                    miu(cur, S_G)
                    need(pe, x5_done, cur, 8)
                    for c in range(CT):
                        project(cur, f"R{c}", Wr, S_R, c * P, (c + 1) * P)
                if mid:
                    need(pe, upd_done, mid, 6)
                    for o in range(2):
                        rows = slice(HD * o, HD * o + HD)
                        lv.wait_free(pe, mid, f"r64_{o}")
                        settle(pe, keep)
                        for ch in range(NC):
                            for c in range(CT):
                                t0, at = ch * P, (ch * CT + c) * 64
                                last = nc.tensor.matmul(lv.tile(f"r64_{o}")[0:64, at:at + 64],
                                                        KG[rows, mid.odd, c, t0:t0 + 64],
                                                        RF[rows, mid.odd, c, t0 + 64:t0 + P], start=True, stop=True)
                        lv.fill(last, f"r64_{o}")
                if cur:
                    need(pe, x5_done, cur, 10)
                    project(cur, "G1a", Wg1, S_G, 0, P)
                    project(cur, "G1b", Wg1, S_G, P, GR)
                if mid:
                    need(pe, upd_done, mid, 7)
                    for c in range(CT):
                        lv.wait_free(pe, mid, f"KT{c}")
                        for ch in range(3):
                            last = nc.tensor.transpose(lv.tile(f"KT{c}")[:, ch * P:(ch + 1) * P],
                                                       KG[:, mid.odd, c, ch * P:(ch + 1) * P], ident[:, :])
                        lv.fill(last, f"KT{c}")
                if mid:
                    lv.wait_drained(pe, mid, "KT1")
                    pj.wait_drained(pe, mid, "V1")
                    lv.wait_free(pe, mid, "KV")
                    for ch in range(3):
                        for h in range(H):
                            at = (ch * CT + h // 2) * HD
                            last = nc.tensor.matmul(lv.tile("KV")[HD * (h % 2):HD * (h % 2) + HD, at:at + HD],
                                                    KGt[:, h // 2, ch * P + HD * (h % 2):ch * P + HD * (h % 2) + HD],
                                                    v[:, mid.odd, ch, h * HD:(h + 1) * HD], start=True, stop=True)
                    lv.fill(last, "KV")
                if old:
                    need(pe, tok_done, old)
                    for c in range(CT):
                        tl.wait_free(pe, old, f"XT{c}")
                        for q in range(NC):
                            last = nc.tensor.transpose(tl.tile(f"XT{c}")[:, q * P:(q + 1) * P],
                                                       tbl[:, old.odd, q, c * P:(c + 1) * P], ident[:, :])
                        tl.fill(last, f"XT{c}")
                if mid:
                    lv.wait_drained(pe, mid, "r64_1")
                    need(pe, acc_copied, mid)
                    lv.wait_drained(pe, mid, "KV")
                    for c in range(CT):
                        lv.wait_free(pe, mid, f"Y{c}")
                        for ch in range(NC):
                            for hh in range(2):
                                h = 2 * c + hh
                                rows = slice(HD * hh, HD * hh + HD)
                                o = lv.tile(f"Y{c}")[rows, ch * P:(ch + 1) * P]
                                last = nc.tensor.matmul(o, v[:, mid.odd, ch, h * HD:(h + 1) * HD], AT[:, (hh * NC + ch) * CT + c, :],
                                                        start=True, stop=(ch == 0))
                                if ch:
                                    last = nc.tensor.matmul(o, S[rows, ch - 1, c, :], RF[rows, mid.odd, c, ch * P:(ch + 1) * P],
                                                            start=False, stop=True)
                        lv.fill(last, f"Y{c}")
                if old:
                    tl.wait_drained(pe, old, "XT1")
                    tl.wait_free(pe, old, "LG")
                    for q in range(NC):
                        for c in range(CT):
                            last = nc.tensor.matmul(tl.tile("LG")[:, q * E:(q + 1) * E], xnT[:, c, q * P:(q + 1) * P],
                                                    Rw[:, c, :], start=(c == 0), stop=(c == CT - 1))
                    tl.fill(last, "LG")

            pipeline(pe, NB, lags, step)

        @block.vector
        def _(dve):
            nc.vector.memset(std[:, :], 0.0).then_inc(const_chain.sem, 1)
            dve.wait_ge(const_chain.sem, 1)
            nc.vector.tensor_copy(rs[:, :].bitcast(F32R), std[:, :]).then_inc(const_chain.sem, 1)
            dve.wait_ge(const_chain.sem, 2)
            nc.vector.memset(BpP[:, :, :], 0.0).then_inc(zeroed.sem, 1)
            nc.vector.memset(AT[:, :, :], 0.0)
            nc.vector.memset(hp[:, :, :, 0:1], 0.0)
            nc.vector.memset(half[:, :], -0.5)
            nc.vector.memset(eps4[:, :], GN_EPS)
            dve.wait_ge(w_in.sem, 16 * n_weights)
            Wv3 = Wv[:, :, :].rearrange("p c (h n) -> p (c h) n", h=H)
            chain = [2]

            def link(i):
                chain[0] += 1
                i.then_inc(const_chain.sem, 1)
                dve.wait_ge(const_chain.sem, chain[0])

            link(nc.vector.tensor_copy(selT[:, :, :].bitcast(F32R), std[:, 0:C].rearrange("h (c p) -> h c p", c=CT)))
            link(nc.vector.tensor_reduce(wsum[:, :], Wv3, AX.X, ALU.add))
            link(nc.vector.tensor_scalar_mul(wsum[:, :], wsum[:, :], 1.0 / HD))
            nc.vector.tensor_tensor(Wv3, Wv3, wsum[:, :].unsqueeze(2).to_broadcast([P, CT * H, HD]), ALU.subtract)\
              .then_inc(const_ok.sem, 1)

            def blend(row, s):
                if s == 0:
                    need(dve, ba_done, row)
                for c in range(CT):
                    n = 2 * s + c
                    pj.wait_filled(dve, row, f"miu{s}{c}")
                    need(dve, x5_done, row, n - T_RING + 1)
                    pj.drain(nc.vector.scalar_tensor_tensor(out=tt[:, n % T_RING, :], in0=pj.tile(f"miu{s}{c}")[:, :],
                                                            scalar=col[:, LAM + s, c:c + 1], in1=ba[:, c, :],
                                                            op0=ALU.add, op1=ALU.mult), f"miu{s}{c}")

            before = (None, None, "lv1_", "lv2_", "lv4_", "lv8_")

            def merge(row, job, n):
                for o in range(2):
                    if n > 1:
                        lv.wait_drained(dve, row, f"{before[n]}{o}")
                    lv.wait_filled(dve, row, f"{job}{o}")
                    level = mask[:, n, :].unsqueeze(1).to_broadcast([P, NC * CT, 32])
                    settle(dve, keep)
                    if n == 1:
                        both = lv.tile(f"{job}{o}")[:, :].rearrange("p (a two t) -> p a two t", two=2, t=32)
                        nc.vector.copy_predicated(acc[:, o * 8:o * 8 + 8, :],
                                                  mask[:, 0, :].unsqueeze(1).to_broadcast([P, NC * CT, 32]),
                                                  both[:, :, 1, :]).then_inc(bonus_in.sem, 1)
                        need(dve, bonus_in, row, o + 1)
                        settle(dve, keep)
                        scores = both[:, :, 0, :]
                    else:
                        scores = lv.tile(f"{job}{o}")[:, 0:256].rearrange("p (a t) -> p a t", t=32)
                    lv.drain(nc.vector.copy_predicated(acc[:, o * 8:o * 8 + 8, :], level, scores), f"{job}{o}")

            def double(row, L):
                k = {1: 1, 2: 2, 4: 3, 8: 4, 16: 5, 32: 6, 64: 7}[L]
                f = d[:, row.odd, :, :] if L == 1 else full[L][:, :, :]
                f2 = f.rearrange("p c (n two) -> p (c n) two", two=2)
                K4 = KG[:, row.odd, :, :].rearrange("p c (n two l) -> p (c n) two l", two=2, l=L)
                R4 = RF[:, row.odd, :, :].rearrange("p c (n two l) -> p (c n) two l", two=2, l=L)
                n = CT * T // (2 * L)
                if k > 1:
                    need(dve, upd_done, row, k - 1)
                nc.vector.tensor_tensor(K4[:, :, 0, :], K4[:, :, 0, :], f2[:, :, 1:2].to_broadcast([P, n, L]), ALU.mult)
                nc.vector.tensor_tensor(R4[:, :, 1, :], R4[:, :, 1, :], f2[:, :, 0:1].to_broadcast([P, n, L]), ALU.mult)
                nc.vector.tensor_tensor(full[2 * L][:, :, :].rearrange("p c n -> p (c n)"), f2[:, :, 0], f2[:, :, 1],
                                        ALU.mult).then_inc(upd_done.sem, 1)

            def step(nxt, cur, mid, old):
                if mid:
                    lv.wait_filled(dve, mid, "lv1_1")
                    double(mid, 1)
                    need(dve, acc_zero, mid)
                    merge(mid, "lv1_", 1)
                if cur:
                    blend(cur, S_W)
                if mid:
                    lv.wait_filled(dve, mid, "lv2_1")
                    double(mid, 2)
                    merge(mid, "lv2_", 2)
                if cur:
                    blend(cur, S_K)
                if old:
                    tl.wait_drained(dve, old, "SS")
                    tl.wait_filled(dve, old, "RB1", back=1)
                    nc.vector.reciprocal(std[0:H, :], std[0:H, :]).then_inc(rs_step.sem, 1)
                    need(dve, rs_step, old, 1)
                    high_part(nc, rs[0:H, :], std[0:H, :]).then_inc(rs_step.sem, 1)
                    need(dve, rs_step, old, 2)
                    low_part(nc.vector, rs[32:HL, :], std[0:H, :], rs[0:H, :]).then_inc(rs_done.sem, 1)
                if mid:
                    lv.wait_filled(dve, mid, "lv4_1")
                    double(mid, 4)
                    merge(mid, "lv4_", 3)
                if cur:
                    blend(cur, S_V)
                if old:
                    for c in range(CT):
                        tl.wait_filled(dve, old, f"RB{c}")
                        tl.drain(nc.vector.tensor_tensor(gn[:, c, :], ys[:, c, :], tl.tile(f"RB{c}")[:, :], ALU.mult),
                                 f"RB{c}")
                    lv.wait_drained(dve, old, "G21")
                    for c in range(CT):
                        tl.wait_drained(dve, old, f"RB{c}")
                        nc.vector.scalar_tensor_tensor(out=gn[:, c, :], in0=gn[:, c, :], scalar=col[:, BETA, c:c + 1],
                                                       in1=gT[:, old.odd, c, :], op0=ALU.add, op1=ALU.mult)\
                          .then_inc(gn_done.sem, 1)
                if mid:
                    lv.wait_filled(dve, mid, "lv8_1")
                    double(mid, 8)
                    merge(mid, "lv8_", 4)
                if cur:
                    lv.wait_filled(dve, cur, "KT1", back=2)
                    for c in range(CT):
                        pj.wait_drained(dve, cur, f"tdB{c}")
                        pj.wait_filled(dve, cur, f"K{c}")
                        pj.drain(nc.vector.scalar_tensor_tensor(out=KG[:, cur.odd, c, :], in0=d[:, cur.odd, c, :], scalar=1.0,
                                                                in1=pj.tile(f"K{c}")[:, :], op0=ALU.min, op1=ALU.mult),
                                 f"K{c}")
                    blend(cur, S_R)
                if old:
                    need_dma(dve, x_in, old)
                    need(dve, xm_out, old, back=1)
                    for j in range(2):
                        tl.wait_filled(dve, old, f"WO{j}")
                        tl.drain(nc.vector.tensor_tensor(xm[:, 2 * j:2 * j + 2, :], x[:, old.odd, 2 * j:2 * j + 2, :],
                                                         tl.tile(f"WO{j}")[:, :].rearrange("p (a d) -> p a d", a=2), ALU.add),
                                 f"WO{j}")
                    tl.wait_drained(dve, old, "WO1")
                    for q in range(NC):
                        last = nc.vector.bn_stats(stats[:, q, :], xm[:, q, :])
                    last.then_inc(st_done.sem, 1)
                if mid:
                    lv.wait_filled(dve, mid, "lv16_1")
                    double(mid, 16)
                    merge(mid, "lv16_", 5)
                if old:
                    need(dve, st_done, old)
                    settle(dve, keep)
                    for q in range(NC):
                        last = nc.vector.bn_aggr(mv[:, q, :], stats[:, q, :])
                    last.then_inc(mv_done.sem, 1)
                    need(dve, mv_done, old)
                    nc.vector.tensor_scalar_add(var[:, :], mv[:, :, 1], LN_EPS).then_inc(var_done.sem, 1)
                if mid:
                    lv.wait_filled(dve, mid, "r32_1")
                    double(mid, 32)
                if old:
                    need(dve, rstd_done, old)
                    for q in range(NC):
                        last = nc.vector.tensor_scalar(xh[:, q, :], xm[:, q, :], mv[:, q, 0:1], rstd[:, q:q + 1],
                                                       ALU.subtract, ALU.mult)
                    last.then_inc(xh_done.sem, 1)
                    need(dve, xh_done, old)
                    need(dve, ms_done, old, back=1)
                    need(dve, tok_done, old, back=1)
                    nc.vector.tensor_tensor(h2[:, :, :], xh[:, :, :], mb[:, old.odd, CB:CB + 1, :].to_broadcast([P, NC, C]),
                                            ALU.mult).then_inc(h2a_done.sem, 1)
                if cur:
                    blend(cur, S_G)
                if old:
                    need(dve, ms_done, old)
                    nc.vector.tensor_scalar(msr[:, :], ms[:, :], 1.0 / C, RMS_EPS, ALU.mult, ALU.add)\
                      .then_inc(msr_done.sem, 1)
                if mid:
                    lv.wait_filled(dve, mid, "r64_1")
                    need(dve, s_step, mid, back=1)
                    lv.wait_drained(dve, mid, "KV", back=1)
                    double(mid, 64)
                if old:
                    need(dve, rr_done, old)
                    need_dma(dve, tbl_out, old, back=2)
                    for q in range(NC):
                        last = nc.vector.scalar_tensor_tensor(out=tbl[:, old.odd, q, 0:C], in0=h2[:, q, :],
                                                              scalar=rr[:, q:q + 1], in1=nw[:, :],
                                                              op0=ALU.mult, op1=ALU.mult)
                    last.then_inc(tok_done.sem, 1)
                if mid:
                    lv.wait_filled(dve, mid, "KV")
                    kv = lv.tile("KV")[:, 0:3 * CT * HD].rearrange("p (n c i) -> p n c i", n=3, c=CT)
                    need(dve, upd_done, mid, 7)
                    nc.vector.tensor_copy(S[:, 0, :, :], kv[:, 0, :, :]).then_inc(s_step.sem, 1)
                    for n in (1, 2):
                        need(dve, s_step, mid, n)
                        for c in range(CT):
                            last = nc.vector.scalar_tensor_tensor(out=S[:, n, c, :], in0=S[:, n - 1, c, :],
                                                                  scalar=full[128][:, c, n:n + 1], in1=kv[:, n, c, :],
                                                                  op0=ALU.mult, op1=ALU.add)
                        if n == 1:
                            last.then_inc(s_step.sem, 1)
                    lv.drain(last, "KV")
                if old:
                    tl.wait_filled(dve, old, "LG")
                    need(dve, kept, old, back=1)
                    tl.drain(nc.vector.tensor_tensor(lgt[:, :, :], tl.tile("LG")[:, 0:NC * E].rearrange("p (q e) -> p q e", e=E),
                                                     rb[:, :].unsqueeze(1).to_broadcast([P, NC, E]), ALU.add), "LG")
                    tl.wait_drained(dve, old, "LG")
                    nc.vector.tensor_reduce(lmx[:, :], lgt[:, :, :], AX.X, ALU.max).then_inc(soft.sem, 1)
                    need(dve, soft, old, 1)
                    nc.vector.tensor_tensor(lsh[:, :, :], lgt[:, :, :], lmx[:, :].unsqueeze(2).to_broadcast([P, NC, E]),
                                            ALU.subtract).then_inc(soft.sem, 1)
                    need(dve, exp_done, old)
                    nc.vector.tensor_reduce(lsum[:, :], lex[:, :, :], AX.X, ALU.add).then_inc(soft.sem, 1)
                    need(dve, soft, old, 3)
                    nc.vector.reciprocal(lrc[:, :], lsum[:, :]).then_inc(soft.sem, 1)
                    need(dve, soft, old, 4)
                    nc.vector.tensor_tensor(tbl[:, old.odd, :, C:TW], lex[:, :, :],
                                            lrc[:, :].unsqueeze(2).to_broadcast([P, NC, E]), ALU.mult).then_inc(soft.sem, 1)

            pipeline(dve, NB, lags, step)

        @block.gpsimd
        def _(pool):
            pool.wait_ge(const_ok.sem, 1)

            def add(row, s):
                slot = X5_SLOT[s]
                if s < 3:
                    pj.wait_filled(pool, row, {0: "R1", 1: "G1b", 2: "V1"}[s], back=1)
                else:
                    pj.wait_filled(pool, row, {3: "tdA", 4: "K1"}[s])
                for c in range(CT):
                    pj.wait_drained(pool, row, f"miu{s}{c}")
                    nc.gpsimd.tensor_tensor(x5[:, slot, c, :], tt[:, (2 * s + c) % T_RING, :], hp[:, row.odd, c, 1:T + 1],
                                            ALU.add).then_inc(x5_done.sem, 1)

            def step(nxt, cur, mid, old):
                if cur:
                    need_dma(pool, H_in, cur)
                    pj.wait_filled(pool, cur, "Ht1", back=1)
                    settle(pool, keep)
                    nc.gpsimd.tensor_copy(Hr[:, :, :, :], Hs[:, cur.odd, :, :].rearrange("p s (i k) -> p i s k", i=4))\
                      .then_inc(Hr_done.sem, 1)
                if mid:
                    need(pool, acc_copied, mid, back=1)
                    settle(pool, keep)
                    nc.gpsimd.memset(acc[:, :, :], 0.0).then_inc(acc_zero.sem, 1)
                if cur:
                    need_dma(pool, h_in, cur)
                    pj.wait_drained(pool, cur, "miu41", back=1)
                    for c in range(CT):
                        last = nc.gpsimd.tensor_tensor(ba[:, c, :], hp[:, cur.odd, c, 0:T], hp[:, cur.odd, c, 1:T + 1],
                                                       ALU.subtract)
                    last.then_inc(ba_done.sem, 1)
                if old:
                    need_dma(pool, x_in, old)
                    tl.wait_filled(pool, old, "WO1", back=1)
                    nc.gpsimd.tensor_tensor(WoG[:, :, :], Wo[:, :, :], mb[:, old.odd, GA:GA + 1, :].to_broadcast([P, CT, C]),
                                            ALU.mult).then_inc(wog_done.sem, 1)
                if cur:
                    add(cur, S_W)
                    add(cur, S_K)
                    add(cur, S_V)
                    add(cur, S_R)
                if old:
                    need(pool, var_done, old)
                    nc.gpsimd.tensor_tensor(rstd[:, :], var[:, :], half[:, :], ALU.pow).then_inc(rstd_done.sem, 1)
                if old:
                    need(pool, h2a_done, old)
                    nc.gpsimd.tensor_tensor(h2[:, :, :], h2[:, :, :], mb[:, old.odd, SB:SB + 1, :].to_broadcast([P, NC, C]),
                                            ALU.add).then_inc(h2_done.sem, 1)
                if cur:
                    add(cur, S_G)
                if cur:
                    pj.wait_drained(pool, cur, "R1")
                    lv.wait_filled(pool, cur, "lv1_1", back=1)
                    settle(pool, keep)
                    for c in range(CT):
                        last = nc.gpsimd.tensor_scalar(RF[:, 2, c, :], RF[:, cur.odd, c, :], col[:, BONUS, c:c + 1], None,
                                                       ALU.mult)
                    last.then_inc(ru_done.sem, 1)
                if old:
                    need(pool, msr_done, old)
                    nc.gpsimd.tensor_tensor(rr[:, :], msr[:, :], half[:, :], ALU.pow).then_inc(rr_done.sem, 1)
                    tl.wait_drained(pool, old, "LG")
                    settle(pool, keep)
                    nc.gpsimd.tensor_copy(keep["logits"][:, bass.ds(old.n * (NC * E), NC * E)],
                                          lgt[:, :, :].rearrange("p q e -> p (q e)")).then_inc(kept.sem, 1)

            pipeline(pool, NB, lags, step)

        @block.scalar
        def _(act):
            act.wait_ge(const_ok.sem, 1)

            def step(nxt, cur, mid, old):
                if cur:
                    pj.wait_filled(act, cur, "miu41", back=1)
                    for j, o in ((0, hs[:, :]), (1, hs4[:, :])):
                        pj.wait_filled(act, cur, f"Ht{j}")
                        pj.drain(nc.scalar.activation(o.rearrange("k (p i) -> k i p", i=4),
                                                      pj.tile(f"Ht{j}")[0:o.shape[0], :].rearrange("k (i p) -> k i p", i=4),
                                                      ACT.Copy), f"Ht{j}")
                if old:
                    tl.wait_filled(act, old, "SS")
                    need(act, rs_done, old, back=1)
                    tl.drain(nc.scalar.activation(std[0:H, :], tl.tile("SS")[0:H, :], ACT.Sqrt, bias=eps4[:, :]), "SS")
                if cur:
                    pj.wait_filled(act, cur, "tdA")
                    pj.drain(nc.scalar.activation(tw[:, :], pj.tile("tdA")[0:WR, :], ACT.Tanh), "tdA")
                    need(act, upd_done, cur, 1, back=2)
                    for c in range(CT):
                        pj.wait_filled(act, cur, f"tdB{c}")
                        pj.drain(nc.scalar.activation(d[:, cur.odd, c, :], pj.tile(f"tdB{c}")[:, :], ACT.Exp,
                                                      bias=col[:, TDMIU, c:c + 1]), f"tdB{c}")
                    lv.wait_filled(act, cur, "Y1", back=2)
                    for j in range(2):
                        pj.wait_filled(act, cur, f"V{j}")
                        pj.drain(nc.scalar.activation(v[:, cur.odd, 2 * j:2 * j + 2, :],
                                                      pj.tile(f"V{j}")[:, :].rearrange("p (a d) -> p a d", a=2),
                                                      ACT.Copy), f"V{j}")
                if mid:
                    lv.wait_filled(act, mid, "Y1", back=1)
                    for o in range(2):
                        lv.wait_filled(act, mid, f"r32_{o}")
                        for pr in range(2):
                            rows = slice(64 * pr, 64 * pr + 32)
                            last = nc.scalar.activation(AT[rows, 8 * o:8 * o + 8, 64 * pr + 32:64 * pr + 64],
                                                        lv.tile(f"r32_{o}")[rows, 0:256].rearrange("p (a t) -> p a t", t=32),
                                                        ACT.Copy)
                        lv.drain(last, f"r32_{o}")
                    need(act, gn_done, mid, back=2)
                    for c in range(CT):
                        lv.wait_filled(act, mid, f"G2{c}")
                        lv.drain(nc.scalar.activation(gT[:, mid.odd, c, :], lv.tile(f"G2{c}")[:, :], ACT.Copy), f"G2{c}")
                if cur:
                    for c in range(CT):
                        pj.wait_filled(act, cur, f"R{c}")
                        pj.drain(nc.scalar.activation(RF[:, cur.odd, c, :], pj.tile(f"R{c}")[:, :], ACT.Copy), f"R{c}")
                if old:
                    need(act, h2_done, old)
                    need(act, ms_done, old, back=1)
                    for q in range(NC):
                        last = nc.scalar.activation(xh[:, q, :], h2[:, q, :], ACT.Square, accum_out=ms[:, q:q + 1])
                    last.then_inc(ms_done.sem, 1)
                if mid:
                    for j in range(2):
                        lv.wait_filled(act, mid, f"r64_{j}")
                        lv.drain(nc.scalar.activation(AT[0:64, 8 * j:8 * j + 8, 64:P],
                                                      lv.tile(f"r64_{j}")[0:64, :].rearrange("p (a t) -> p a t", t=64),
                                                      ACT.Copy), f"r64_{j}")
                if cur:
                    lv.wait_filled(act, cur, "G21", back=2)
                    pj.wait_filled(act, cur, "G1a")
                    pj.drain(nc.scalar.activation(tg[:, cur.odd, :], pj.tile("G1a")[:, :], ACT.Tanh), "G1a")
                    pj.wait_filled(act, cur, "G1b")
                    pj.drain(nc.scalar.activation(tgb[:, cur.odd, :], pj.tile("G1b")[0:GR - P, :], ACT.Tanh), "G1b")
                if mid:
                    for c in range(CT):
                        lv.wait_filled(act, mid, f"KT{c}")
                        lv.drain(nc.scalar.activation(KGt[:, c, :], lv.tile(f"KT{c}")[:, 0:3 * P], ACT.Copy), f"KT{c}")
                    lv.wait_drained(act, mid, "lv16_0")
                    lv.wait_drained(act, mid, "lv16_1")
                    for q in range(4):
                        rows = slice(32 * q, 32 * q + 32)
                        last = nc.scalar.activation(AT[rows, :, 32 * q:32 * q + 32], acc[rows, :, :], ACT.Copy)
                    last.then_inc(acc_copied.sem, 1)
                if old:
                    for c in range(CT):
                        tl.wait_filled(act, old, f"XT{c}")
                        tl.drain(nc.scalar.activation(xnT[:, c, :], tl.tile(f"XT{c}")[:, :], ACT.Copy), f"XT{c}")
                if mid:
                    tl.wait_drained(act, mid, "RB1", back=1)
                    tl.wait_filled(act, mid, "SS", back=1)
                    for c in range(CT):
                        lv.wait_filled(act, mid, f"Y{c}")
                        nc.scalar.activation(ys[:, c, :], lv.tile(f"Y{c}")[:, :], ACT.Copy, scale=col[:, GAMMA, c:c + 1])
                        lv.drain(nc.scalar.activation(ysq[:, c, :], lv.tile(f"Y{c}")[:, :], ACT.Square), f"Y{c}")
                if old:
                    need(act, soft, old, 2)
                    nc.scalar.activation(lex[:, :, :], lsh[:, :, :], ACT.Exp).then_inc(exp_done.sem, 1)

            pipeline(act, NB, lags, step)


SEG = P // E


def rank(nc, ins, dram, keep, NB):
    NT = NB * NC
    G = NT // SEG
    W = G * P
    TOPK = NB * T // E
    with ExitStack() as ctx:
        def sb(name, shape, dt=F32):
            return ctx.enter_context(nc.sbuf_tensor(name, shape, dt))

        def sem(name):
            return ctx.enter_context(nc.semaphore(name))

        grouped = sb("grouped", [P, G, SEG, E])
        L8 = sb("L8", [P, W])
        taken = sb("taken", [P, W])
        equal = sb("equal", [P, W])
        run = sb("run", [P, W])
        ones = sb("ones", [P, W])
        same = sb("same", [P, P])
        before = sb("before", [P, P])
        cnt = sb("cnt", [P, 1])
        cur = sb("cur", [P, 1], I32)
        cand = sb("cand", [P, 1], I32)
        bit = sb("bit", [P, 1], I32)
        signbit = sb("signbit", [P, 1], I32)
        neg = sb("neg", [P, 1])
        negi = sb("negi", [P, 1], I32)
        accept = sb("accept", [P, 1], I32)
        room = sb("room", [P, 1])
        off = sb("off", [P, 1])
        nb = max(1, W // 512)
        psT = [ctx.enter_context(nc.psum_tensor(f"psT{k}", [P, 512], F32)) for k in range(nb)]
        psN = ctx.enter_context(nc.psum_tensor("psN", [P, 8], F32))
        loaded, grouped_done, turned, chain = sem("rk_loaded"), sem("rk_grouped"), sem("rk_turned"), sem("rk_chain")
        counted, summed, stored = sem("rk_counted"), sem("rk_summed"), sem("rk_stored")
        ranked = sem("rk_ranked")
        block = ctx.enter_context(nc.Block())
        BITS = 31
        STEPS = 4

        @block.sync
        def _(sp):
            sp.dma_start(same[:, :], ins["same"]).then_inc(loaded, 16)
            sp.dma_start(before[:, :], ins["before"]).then_inc(loaded, 16)
            sp.wait_ge(ranked, 1)
            for j in range(SEG):
                sp.dma_start(dram["count"][:, j * W:(j + 1) * W], run[j * E:(j + 1) * E, :]).then_inc(stored, 16)
            sp.wait_ge(stored, 16 * SEG)

        @block.tensor
        def _(pe):
            pe.wait_ge(loaded, 32)
            pe.wait_ge(grouped_done, 1)
            for g in range(G):
                last = nc.tensor.transpose(psT[g // 4][:, (g % 4) * P:(g % 4 + 1) * P],
                                           grouped[:, g, :, :].rearrange("p j e -> p (j e)"), keep["ident"][:, :])
            last.then_inc(turned, 1)
            pe.wait_ge(counted, 1)
            nc.tensor.matmul(psN[:, 0:1], same[:, :], cnt[:, :], start=True, stop=True).then_inc(summed, 1)
            with pe.Fori(0, BITS) as n:
                pe.wait_ge(counted, n + 2)
                nc.tensor.matmul(psN[:, 0:1], same[:, :], cnt[:, :], start=True, stop=True).then_inc(summed, 1)
            pe.wait_ge(counted, BITS + 2)
            nc.tensor.matmul(psN[:, 0:1], same[:, :], cnt[:, :], start=True, stop=True).then_inc(summed, 1)
            pe.wait_ge(counted, BITS + 3)
            nc.tensor.matmul(psN[:, 0:1], before[:, :], run[:, W - 1:W], start=True, stop=True).then_inc(summed, 1)
            pe.wait_ge(counted, BITS + 4)
            nc.tensor.matmul(psN[:, 0:1], before[:, :], run[:, W - 1:W], start=True, stop=True).then_inc(summed, 1)

        @block.vector
        def _(dve):
            state = {"n": 0}

            def link(i, base=0):
                state["n"] += 1
                i.then_inc(chain, 1)
                dve.wait_ge(chain, base + state["n"])

            nc.vector.tensor_copy(grouped[:, :, :, :],
                                  keep["logits"][:, 0:NT * E].rearrange("p (j g e) -> p g j e", j=SEG, g=G)).then_inc(grouped_done, 1)
            nc.vector.memset(ones[:, :], 1.0)
            nc.vector.memset(signbit[:, :], -2 ** 31)
            nc.vector.memset(cur[:, :], 0)
            link(nc.vector.memset(bit[:, :], 2 ** 30))
            dve.wait_ge(turned, 1)
            for k in range(nb):
                w = min(512, W)
                last = nc.vector.tensor_copy(L8[:, k * w:(k + 1) * w], psT[k][:, 0:w])
            link(last)
            nc.vector.tensor_scalar(taken[:, :], L8[:, :], 0.0, None, ALU.is_ge, ALU.add, accum_out=cnt[:, :])\
              .then_inc(counted, 1)
            dve.wait_ge(summed, 1)
            link(nc.vector.tensor_scalar(neg[:, :], psN[:, 0:1], float(TOPK), None, ALU.is_lt))
            link(nc.vector.tensor_copy(negi[:, :], neg[:, :]))
            link(nc.vector.copy_predicated(cur[:, :], negi[:, :], signbit[:, :]))
            base = state["n"]
            with dve.Fori(0, BITS) as n:
                state["n"] = 0
                at = n * STEPS + base
                link(nc.vector.tensor_tensor(cand[:, :], cur[:, :], bit[:, :], ALU.bitwise_or), at)
                nc.vector.tensor_scalar(taken[:, :], L8[:, :], cand[:, :].bitcast(F32), None, ALU.is_ge, ALU.add,
                                        accum_out=cnt[:, :]).then_inc(counted, 1)
                link(nc.vector.tensor_scalar(bit[:, :], bit[:, :], 1, None, ALU.logical_shift_right), at)
                dve.wait_ge(summed, n + 2)
                link(nc.vector.tensor_scalar(accept[:, :], psN[:, 0:1], float(TOPK), neg[:, :], ALU.is_ge,
                                             ALU.not_equal), at)
                settle(dve, keep)
                link(nc.vector.copy_predicated(cur[:, :], accept[:, :], cand[:, :]), at)
                assert state["n"] == STEPS
            state["n"] = base + BITS * STEPS
            link(nc.vector.tensor_tensor(cur[:, :], cur[:, :], negi[:, :], ALU.add))
            thr = cur[:, :].bitcast(F32)
            nc.vector.tensor_scalar(taken[:, :], L8[:, :], thr, None, ALU.is_gt, ALU.add, accum_out=cnt[:, :])\
              .then_inc(counted, 1)
            link(nc.vector.tensor_scalar(equal[:, :], L8[:, :], thr, None, ALU.is_equal))
            dve.wait_ge(summed, BITS + 2)
            link(nc.vector.tensor_scalar(room[:, :], psN[:, 0:1], -1.0, float(TOPK), ALU.mult, ALU.add))
            nc.vector.tensor_tensor_scan(run[:, :], ones[:, :], equal[:, :], 0.0, ALU.mult, ALU.add).then_inc(counted, 1)
            dve.wait_ge(counted, BITS + 3)
            dve.wait_ge(summed, BITS + 3)
            link(nc.vector.tensor_tensor(room[:, :], room[:, :], psN[:, 0:1], ALU.subtract))
            link(nc.vector.scalar_tensor_tensor(out=equal[:, :], in0=run[:, :], scalar=room[:, :], in1=equal[:, :],
                                                op0=ALU.is_le, op1=ALU.mult))
            link(nc.vector.tensor_tensor(taken[:, :], taken[:, :], equal[:, :], ALU.add))
            nc.vector.tensor_tensor_scan(run[:, :], ones[:, :], taken[:, :], 0.0, ALU.mult, ALU.add).then_inc(counted, 1)
            dve.wait_ge(counted, BITS + 4)
            dve.wait_ge(summed, BITS + 4)
            link(nc.vector.tensor_copy(off[:, :], psN[:, 0:1]))
            nc.vector.tensor_scalar(run[:, :], run[:, :], off[:, :], None, ALU.add).then_inc(ranked, 1)


def experts(nc, ins, dram, keep, NB):
    NT = NB * NC
    TOPK = NB * T // E
    BLK = TOPK // P
    TB = min(512, TOPK)
    HALVES = TOPK // TB
    PER = TB // P
    with ExitStack() as ctx:
        def sb(name, shape, dt=F32):
            return ctx.enter_context(nc.sbuf_tensor(name, shape, dt))

        def sig(name, per=1, unit=1):
            return Signal(ctx.enter_context(nc.semaphore(name)), per, unit)

        ident = keep["ident"]
        count = sb("count", [NT, E, P])
        ends = sb("ends", [NT, E])
        starts = sb("starts", [NT, E])
        shift = sb("shiftm", [P, P])
        slot_row = sb("slot_row", [NT, TOPK])
        slot_col = sb("slot_col", [P, BLK])
        hit = sb("hit", [P, TOPK])
        onehot = sb("onehot", [NT, TOPK])
        tile_count = sb("tile_count", [NT, 2, P + 1])
        place = sb("place", [P, BLK])
        tile_of = sb("tile_of", [P, BLK])
        token = sb("token", [P, 2, BLK], mybir.dt.uint32)
        rows = sb("rows_in", [P, 2, BLK, TW])
        gate = sb("gate", [P, 2, BLK])
        w1 = sb("w1", [P, CT, F])
        b1 = sb("b1", [P, 2, FT])
        w2 = sb("w2", [P, FT, C])
        b2 = sb("b2", [P, 2, C])
        w1_high = sb("w1_high", [P, CT, F])
        w1_low = sb("w1_low", [P, CT, F])
        w2_high = sb("w2_high", [P, FT, C])
        w2_low = sb("w2_low", [P, FT, C])
        x_low = sb("x_low", [P, CT, TOPK])
        x_high = sb("x_high", [P, CT, TOPK])
        h_raw = keep["logits"][:, 0:4 * TB].rearrange("p (r f t) -> p r f t", r=2, f=2)
        h_low = sb("h_low", [P, FT, TOPK])
        h_high = sb("h_high", [P, FT, TOPK])
        ysum = sb("ysum", [P, BLK, C])
        out = sb("out_rows", [P, 2, BLK, AW])
        IX = (BLK + 2) // 3
        ixb = Banks(ctx, nc, 0, 2, [f"IX{j}" for j in range(IX)] if IX > 1 else ["IX0", "unused"], "ix")
        YJ = (BLK + 1) // 2
        xb = Banks(ctx, nc, 2, 6, [f"X{c}{g}" for g in range(HALVES) for c in range(CT)] +
                   [f"H{g}{f}" for g in range(HALVES) for f in range(FT)] + [f"Y{j}" for j in range(YJ)], "xb")

        c_in = sig("ex_const_in")
        w_in = [sig(f"ex_w_in{k}", 4) for k in range(2)]
        ready, range_done, hit_done, onehot_done = sig("ex_ready"), sig("ex_ranges"), sig("hit_done"), sig("onehot_done")
        token_done = sig("token_done")
        xh_done, hh_done, h_split = sig("x_high_done", CT * HALVES), sig("h_high_done", FT * HALVES // 2), sig("h_split", FT * HALVES // 2)
        w1h_done, w1_split, w2h_done, w2_split = sig("w1_high_done"), sig("w1_split"), sig("w2_high_done"), sig("w2_split")
        gathered = [sig(f"gathered{k}", BLK) for k in range(2)]
        gate_done, out_done = sig("gate_done"), sig("out_done", BLK)
        scattered = [sig(f"scattered{k}", BLK) for k in range(2)]
        block = ctx.enter_context(nc.Block())
        lags = (0, 1, 2)

        @block.sync
        def _(sp):
            sp.dma_start(count[:, :, :], dram["count"].rearrange("e (n p) -> n e p", p=P)).then_inc(c_in.sem, 16)
            sp.dma_start(shift[:, :], ins["shift"]).then_inc(c_in.sem, 16)
            sp.dma_start(slot_row[:, :], ins["slot_row"].to_broadcast([NT, TOPK])).then_inc(c_in.sem, 16)
            sp.dma_start(slot_col[:, :], ins["slot_col"]).then_inc(c_in.sem, 16)
            for k in range(2):
                sp.dma_start(tile_count[:, k, P:P + 1], ins["tile_id"][0:NT, :]).then_inc(c_in.sem, 16)

            def step(nxt, cur, mid):
                if nxt:
                    xb.wait_filled(sp, nxt, f"Y{YJ - 1}", back=2)
                    xb.wait_drained(sp, nxt, f"Y{YJ - 1}", back=2)
                    settle(sp, keep)
                    o = nxt.odd
                    need(sp, w1_split, nxt, back=1)
                    settle(sp, keep)
                    sp.dma_start(w1[:, :, :], ins["fc1T"][nxt.n].rearrange("(c p) f -> p c f", p=P)).then_inc(w_in[o].sem, 16)
                    sp.dma_start(b1[:, o, :], ins["fc1b"][nxt.n]).then_inc(w_in[o].sem, 16)
                    need(sp, w2_split, nxt, back=1)
                    settle(sp, keep)
                    sp.dma_start(w2[:, :, :], ins["fc2T"][nxt.n].rearrange("(f p) d -> p f d", p=P)).then_inc(w_in[o].sem, 16)
                    sp.dma_start(b2[:, o, :], ins["fc2b"][nxt.n].to_broadcast([P, C])).then_inc(w_in[o].sem, 16)

            pipeline(sp, E, lags, step)

        @block.tensor
        def _(pe):
            pe.wait_ge(c_in.sem, 16 * 6)
            pe.wait_ge(ready.sem, 1)
            nc.tensor.matmul(ixb.tile("IX0")[0:NT, 0:E], shift[0:NT, 0:NT], ends[:, :], start=True, stop=True)\
              .then_inc(ready.sem, 1)

            def tiles_of(cur, g):
                if g == 0:
                    need(pe, onehot_done, cur)
                    if isinstance(cur.n, int) and cur.n == 0:
                        pe.wait_ge(range_done.sem, 1)
                for j in range(IX):
                    if min(j // 2, HALVES - 1) == g:
                        ixb.wait_free(pe, cur, f"IX{j}")
                        for k in range(3 * j, min(3 * j + 3, BLK)):
                            last = nc.tensor.matmul(ixb.tile(f"IX{j}")[:, (k % 3) * (P + 1):(k % 3 + 1) * (P + 1)],
                                                    onehot[:, k * P:(k + 1) * P], tile_count[:, cur.odd, :],
                                                    start=True, stop=True)
                        ixb.fill(last, f"IX{j}")

            def step(nxt, cur, mid):
                if cur and not mid:
                    for g in range(HALVES):
                        tiles_of(cur, g)
                if mid:
                    need_dma(pe, gathered, mid)
                    for g in range(HALVES):
                        for c in range(CT):
                            xb.wait_free(pe, mid, f"X{c}{g}")
                            for k in range(PER):
                                last = nc.tensor.transpose(xb.tile(f"X{c}{g}")[:, k * P:(k + 1) * P],
                                                           rows[:, mid.odd, g * PER + k, c * P:(c + 1) * P], ident[:, :])
                            xb.fill(last, f"X{c}{g}")
                    need(pe, w1_split, mid)
                    for g in range(HALVES):
                        xb.wait_drained(pe, mid, f"X1{g}")
                        for f in range(FT):
                            xb.wait_free(pe, mid, f"H{g}{f}")
                            n = 0
                            for c in range(CT):
                                for w, x in ((w1_high, x_high), (w1_high, x_low), (w1_low, x_high)):
                                    last = nc.tensor.matmul(xb.tile(f"H{g}{f}")[:, 0:TB],
                                                            w[:, c, f * P:(f + 1) * P].bitcast(F32R),
                                                            x[:, c, g * TB:(g + 1) * TB].bitcast(F32R),
                                                            start=(n == 0), stop=(n == 3 * CT - 1))
                                    n += 1
                            xb.fill(last, f"H{g}{f}")
                    if cur:
                        tiles_of(cur, 0)
                    need(pe, w2_split, mid)
                    for j in range(YJ):
                        if 2 * j % PER == 0:
                            need(pe, h_split, mid, (2 * j // PER + 1) * (FT // 2))
                        xb.wait_free(pe, mid, f"Y{j}")
                        for k in range(2 * j, min(2 * j + 2, BLK)):
                            n = 0
                            for f in range(FT):
                                for h, w in ((h_high, w2_high), (h_low, w2_high), (h_high, w2_low)):
                                    last = nc.tensor.matmul(xb.tile(f"Y{j}")[:, (k % 2) * C:(k % 2 + 1) * C],
                                                            h[:, f, k * P:(k + 1) * P].bitcast(F32R),
                                                            w[:, f, :].bitcast(F32R),
                                                            start=(n == 0), stop=(n == 3 * FT - 1))
                                    n += 1
                        xb.fill(last, f"Y{j}")
                        if cur and j == 0 and HALVES > 1:
                            tiles_of(cur, 1)

            pipeline(pe, E, lags, step)

        @block.vector
        def _(dve):
            dve.wait_ge(c_in.sem, 16 * 6)
            nc.vector.tensor_copy(ends[:, :], count[:, :, P - 1]).then_inc(ready.sem, 1)
            dve.wait_ge(ready.sem, 2)
            nc.vector.tensor_copy(starts[:, :], ixb.tile("IX0")[0:NT, 0:E]).then_inc(range_done.sem, 1)
            dve.wait_ge(range_done.sem, 1)

            def ranges(cur):
                e = bass.ds(cur.n, 1)
                ixb.wait_filled(dve, cur, f"IX{IX - 1}", back=1)
                need(dve, token_done, cur, back=1)
                nc.vector.tensor_scalar(hit[0:NT, :], slot_row[:, :], starts[:, e], None, ALU.is_ge).then_inc(hit_done.sem, 1)
                nc.vector.tensor_copy(tile_count[:, cur.odd, 0:P].unsqueeze(1), count[:, e, :])
                need(dve, hit_done, cur)
                nc.vector.scalar_tensor_tensor(out=onehot[:, :], in0=slot_row[:, :], scalar=ends[:, e], in1=hit[0:NT, :],
                                               op0=ALU.is_lt, op1=ALU.mult).then_inc(onehot_done.sem, 1)

            def tokens(cur):
                need(dve, onehot_done, cur)
                need_dma(dve, scattered, cur, back=2)
                for j in range(IX):
                    ixb.wait_filled(dve, cur, f"IX{j}")
                    ks = list(range(3 * j, min(3 * j + 3, BLK)))
                    for k in ks:
                        nc.vector.tensor_scalar(hit[:, k * P:(k + 1) * P],
                                                ixb.tile(f"IX{j}")[:, (k % 3) * (P + 1):(k % 3) * (P + 1) + P],
                                                slot_col[:, k:k + 1], None, ALU.is_le, ALU.add, accum_out=place[:, k:k + 1])
                    src = ixb.tile(f"IX{j}")[:, 0:len(ks) * (P + 1)].rearrange("p (k n) -> p k n", n=P + 1)[:, :, P]
                    ixb.drain(nc.vector.tensor_copy(tile_of[:, ks[0]:ks[-1] + 1], src), f"IX{j}")
                for j in range(IX):
                    ixb.wait_drained(dve, cur, f"IX{j}")
                nc.vector.scalar_tensor_tensor(out=token[:, cur.odd, :], in0=tile_of[:, :], scalar=float(P), in1=place[:, :],
                                               op0=ALU.mult, op1=ALU.add).then_inc(token_done.sem, 1)

            def split_hidden(mid, g):
                for u in range(FT // 2):
                    k = g * FT // 2 + u + 1
                    fs, ts = slice(2 * u, 2 * u + 2), slice(g * TB, (g + 1) * TB)
                    xb.wait_drained(dve, mid, f"H{g}{2 * u}")
                    xb.wait_drained(dve, mid, f"H{g}{2 * u + 1}")
                    high_part(nc, h_high[:, fs, ts], h_raw[:, u % 2, :, :]).then_inc(hh_done.sem, 1)
                    need(dve, hh_done, mid, k)
                    low_part(nc.vector, h_low[:, fs, ts], h_raw[:, u % 2, :, :], h_high[:, fs, ts])\
                      .then_inc(h_split.sem, 1)

            def step(nxt, cur, mid):
                if mid:
                    for g in range(HALVES):
                        for c in range(CT):
                            xb.wait_filled(dve, mid, f"X{c}{g}")
                            src, ts = xb.tile(f"X{c}{g}")[:, 0:TB], slice(g * TB, (g + 1) * TB)
                            high_part(nc, x_high[:, c, ts], src).then_inc(xh_done.sem, 1)
                            need(dve, xh_done, mid, g * CT + c + 1)
                            xb.drain(low_part(nc.vector, x_low[:, c, ts], src, x_high[:, c, ts]), f"X{c}{g}")
                    xb.wait_filled(dve, mid, f"Y{YJ - 1}", back=1)
                    need_dma(dve, w_in, mid)
                    high_part(nc, w2_high[:, :, :], w2[:, :, :]).then_inc(w2h_done.sem, 1)
                    split_hidden(mid, 0)
                if cur:
                    ranges(cur)
                if mid:
                    for g in range(1, HALVES):
                        split_hidden(mid, g)
                    xb.wait_filled(dve, mid, f"H{HALVES - 1}{FT - 1}")
                if cur:
                    need_dma(dve, w_in, cur)
                    high_part(nc, w1_high[:, :, :], w1[:, :, :]).then_inc(w1h_done.sem, 1)
                    tokens(cur)
                if mid:
                    need_dma(dve, gathered, mid)
                    nc.vector.tensor_copy(gate[:, mid.odd, :].unsqueeze(2), rows[:, mid.odd, :, bass.ds(mid.n + C, 1)])\
                      .then_inc(gate_done.sem, 1)
                    need(dve, gate_done, mid)
                    need_dma(dve, scattered, mid, back=2)
                    need(dve, out_done, mid, back=1)
                    for j in range(YJ):
                        ks = list(range(2 * j, min(2 * j + 2, BLK)))
                        xb.wait_filled(dve, mid, f"Y{j}")
                        xb.drain(nc.vector.tensor_tensor(ysum[:, ks[0]:ks[-1] + 1, :],
                                                         xb.tile(f"Y{j}")[:, 0:len(ks) * C].rearrange("p (k d) -> p k d", d=C),
                                                         b2[:, mid.odd, :].unsqueeze(1).to_broadcast([P, len(ks), C]), ALU.add),
                                 f"Y{j}")
                        if j == 0:
                            nc.vector.tensor_copy(out[:, mid.odd, :, C:AW], gate[:, mid.odd, :].unsqueeze(2))
                        xb.wait_drained(dve, mid, f"Y{j}")
                        for k in ks:
                            nc.vector.tensor_scalar(out[:, mid.odd, k, 0:C], ysum[:, k, :], gate[:, mid.odd, k:k + 1], None,
                                                    ALU.mult).then_inc(out_done.sem, 1)

            pipeline(dve, E, lags, step)

        @block.scalar
        def _(act):
            def step(nxt, cur, mid):
                if mid:
                    need_dma(act, w_in, mid)
                    for g in range(HALVES):
                        for f in range(FT):
                            xb.wait_filled(act, mid, f"H{g}{f}")
                            if f % 2 == 0:
                                need(act, h_split, mid, g * FT // 2 + f // 2 - 1)
                            xb.drain(nc.scalar.activation(h_raw[:, f // 2 % 2, f % 2, :], xb.tile(f"H{g}{f}")[:, 0:TB], ACT.Gelu,
                                                          bias=b1[:, mid.odd, f:f + 1]), f"H{g}{f}")

            pipeline(act, E, lags, step)

        @block.gpsimd
        def _(pool):
            def step(nxt, cur, mid):
                if mid:
                    need(pool, w2h_done, mid)
                    low_part(nc.gpsimd, w2_low[:, :, :], w2[:, :, :], w2_high[:, :, :])\
                      .then_inc(w2_split.sem, 1)
                if cur:
                    need(pool, w1h_done, cur)
                    low_part(nc.gpsimd, w1_low[:, :, :], w1[:, :, :], w1_high[:, :, :])\
                      .then_inc(w1_split.sem, 1)
                if cur:
                    need(pool, token_done, cur)
                    xb.wait_filled(pool, cur, f"X1{HALVES - 1}", back=2)
                    need(pool, gate_done, cur, back=2)
                    settle(pool, keep)
                    for k in range(BLK):
                        pool.indirect_dma_start(out=rows[:, cur.odd, k, :], out_offset=None, in_=dram["table"],
                                                in_offset=bass.IndirectOffsetOnAxis(token[:, cur.odd, k:k + 1], 0))\
                            .then_inc(gathered[cur.odd].sem, 16)
                if mid:
                    prev = Row(mid.n - 1, mid.half - 1 + mid.odd, 1 - mid.odd)
                    need_dma(pool, scattered, prev)
                    for k in range(BLK):
                        need(pool, out_done, mid, k + 1)
                        settle(pool, keep)
                        pool.indirect_dma_start(out=dram["acc"], in_=out[:, mid.odd, k, :], in_offset=None,
                                                out_offset=bass.IndirectOffsetOnAxis(token[:, mid.odd, k:k + 1], 0),
                                                compute_op=ALU.add).then_inc(scattered[mid.odd].sem, 16)

            pipeline(pool, E, lags, step)
            for k in range(2):
                pool.wait_ge(scattered[k].sem, 16 * BLK * (E // 2))


def combine(nc, ins, dram, keep, NB):
    with ExitStack() as ctx:
        def sb(name, shape, dt=F32):
            return ctx.enter_context(nc.sbuf_tensor(name, shape, dt))

        def sig(name, per=1, unit=1):
            return Signal(ctx.enter_context(nc.semaphore(name)), per, unit)

        a = sb("a_in", [P, 2, NC, AW])
        xm = sb("xm_fin", [P, 2, NC, C])
        gb = sb("gb", [P, 2, C])
        den = sb("den", [P, NC])
        rec = sb("rec", [P, NC])
        t = sb("t_fin", [P, 2, NC, C])
        o = sb("o_fin", [P, 2, NC, C])
        loaded = [sig(f"cb_in{k}", 3) for k in range(2)]
        stored = [sig(f"cb_out{k}") for k in range(2)]
        den_done, rec_done, t_done, o_done = sig("den_done"), sig("rec_done"), sig("t_done"), sig("o_done")
        block = ctx.enter_context(nc.Block())
        lags = (0, 1)

        @block.sync
        def _(sp):
            def step(nxt, cur):
                if nxt:
                    need(sp, t_done, nxt, back=2)
                    need(sp, o_done, nxt, back=2)
                    k = nxt.odd
                    sp.dma_start(a[:, k, :, :], dram["acc"].rearrange("(b c p) d -> b p c d", c=NC, p=P)[nxt.n])\
                      .then_inc(loaded[k].sem, 16)
                    sp.dma_start(xm[:, k, :, :], dram["xmid"][nxt.n].rearrange("(c p) d -> p c d", p=P)).then_inc(loaded[k].sem, 16)
                    sp.dma_start(gb[:, k, :], dram["mod"][nxt.n, GB:GB + 1, :].to_broadcast([P, C])).then_inc(loaded[k].sem, 16)
                if cur:
                    need(sp, o_done, cur)
                    sp.dma_start(dram["out"][cur.n].rearrange("(c p) d -> p c d", p=P), o[:, cur.odd, :, :])\
                      .then_inc(stored[cur.odd].sem, 16)

            pipeline(sp, NB, lags, step)
            for k in range(2):
                sp.wait_ge(stored[k].sem, 16 * (NB // 2))

        @block.vector
        def _(dve):
            def step(nxt, cur):
                if cur:
                    k = cur.odd
                    need_dma(dve, loaded, cur)
                    nc.vector.scalar_tensor_tensor(out=den[:, :], in0=a[:, k, :, C], scalar=0.0, in1=a[:, k, :, C],
                                                   op0=ALU.is_le, op1=ALU.add).then_inc(den_done.sem, 1)
                    need(dve, den_done, cur)
                    nc.vector.reciprocal(rec[:, :], den[:, :]).then_inc(rec_done.sem, 1)
                    need(dve, rec_done, cur)
                    need(dve, o_done, cur, back=2)
                    for q in range(NC):
                        last = nc.vector.scalar_tensor_tensor(out=t[:, k, q, :], in0=a[:, k, q, 0:C], scalar=rec[:, q:q + 1],
                                                              in1=gb[:, k, :], op0=ALU.mult, op1=ALU.mult)
                    last.then_inc(t_done.sem, 1)

            pipeline(dve, NB, lags, step)

        @block.gpsimd
        def _(pool):
            def step(nxt, cur):
                if cur:
                    k = cur.odd
                    need(pool, t_done, cur)
                    need_dma(pool, stored, cur, back=2)
                    nc.gpsimd.tensor_tensor(o[:, k, :, :], t[:, k, :, :], xm[:, k, :, :], ALU.add).then_inc(o_done.sem, 1)

            pipeline(pool, NB, lags, step)


def scratch(NB):
    return {
        "hT": (NB, C, T), "lora": (NB, T, NS * LR), "mod": (NB, 4, C), "xmid": (NB, T, C),
        "table": (NB * T, TW), "count": (E, NB * T), "acc": (NB * T, AW),
    }


def program(nc, ins, dram, NB):
    with ExitStack() as ctx:
        def sb(name, shape, dt=F32):
            return ctx.enter_context(nc.sbuf_tensor(name, shape, dt))

        keep = {
            "passed": ctx.enter_context(nc.semaphore("waits_passed")),
            "ident": sb("ident", [P, P]), "col": sb("col", [P, NCOL, CT]), "modT": sb("modT", [P, 4, NB]),
            "mask": sb("mask", [P, 6, 32], I32), "logits": sb("logits", [P, max(NB * NC * E, 4 * T)]),
        }
        setup(nc, ins, dram, keep, NB)
        lora(nc, ins, dram, keep, NB)
        mixer(nc, ins, dram, keep, NB)
        rank(nc, ins, dram, keep, NB)
        experts(nc, ins, dram, keep, NB)
        combine(nc, ins, dram, keep, NB)


def layout(d):
    def get(name):
        return np.ascontiguousarray(d["L0_" + name])

    def rows_first(a, *order):
        return np.ascontiguousarray(a.transpose(*order))

    columns = [get("attn_miu_x").reshape(C)] + [get("attn_lam")[s, 0, 0] for s in range(NS)]
    columns += [get("attn_td_miu").reshape(C), get("attn_u").reshape(C), get("attn_gamma"), get("attn_beta")]
    arrays = {
        "x": get("attn_x"), "cT": rows_first(get("c"), 1, 0), "wmod": get("wmod"),
        "col": rows_first(np.stack([v.reshape(CT, P) for v in columns]), 2, 0, 1),
        "A": get("attn_A"), "Bp": get("attn_Bp"), "tdA": get("attn_tdA"), "tdB": get("attn_tdB"),
        "Wg1": get("attn_Wg1"), "Wg2": get("attn_Wg2"),
        "nw": get("ffn_norm_weight").reshape(1, C), "rb": get("ffn_router_bias").reshape(1, E),
        "RwT": rows_first(get("ffn_router_weight"), 1, 0),
        "fc1T": rows_first(get("ffn_fc1_weight"), 0, 2, 1),
        "fc1b": rows_first(get("ffn_fc1_bias").reshape(E, FT, P), 0, 2, 1),
        "fc2T": rows_first(get("ffn_fc2_weight"), 0, 2, 1), "fc2b": get("ffn_fc2_bias").reshape(E, 1, C),
    }
    for name in ("Wk", "Wv", "Wr", "Wo"):
        arrays[name + "T"] = rows_first(get("attn_" + name), 1, 0)
    head_of = np.arange(C).reshape(CT, P) // HD
    one_head = (head_of[:, :, None] == np.arange(H)).astype(np.float32)
    arrays["sel"] = np.ascontiguousarray(one_head.transpose(1, 0, 2)) / np.float32(HD)
    arrays["selT"] = np.ascontiguousarray(one_head.transpose(2, 0, 1))
    topk = arrays["x"].shape[0] * T // E
    p = np.arange(P)
    segment, expert = p // E, p % E
    arrays["same"] = (expert[:, None] == expert[None]).astype(np.float32)
    arrays["before"] = arrays["same"] * (segment[:, None] < segment[None]).astype(np.float32)
    arrays["shift"] = (p[:, None] + 1 == p[None]).astype(np.float32)
    arrays["slot_row"] = np.arange(topk, dtype=np.float32).reshape(1, topk)
    arrays["slot_col"] = np.ascontiguousarray(np.arange(topk, dtype=np.float32).reshape(topk // P, P).T)
    arrays["tile_id"] = p.astype(np.float32).reshape(P, 1)
    return arrays


def kernel(**inputs):
    import concourse.bacc as _bacc
    from concourse import mybir as _mybir
    from concourse.bass_utils import run_bass_kernel_spmd as _run

    nc = _bacc.Bacc("TRN2", target_bir_lowering=False, num_devices=1)
    laid, arrays, ins = layout(inputs), {}, {}
    for name, a in laid.items():
        arrays[f"in_{name}_dram"] = a
        ins[name] = nc.dram_tensor(f"in_{name}_dram", a.shape, _mybir.dt.from_np(a.dtype), kind="ExternalInput").ap()
    batch = laid["x"].shape[0]
    out = nc.dram_tensor("out_0_dram", (batch, T, C), _mybir.dt.float32, kind="ExternalOutput").ap()
    dram = {"out": out}
    for name, shape in scratch(batch).items():
        dram[name] = nc.dram_tensor(f"scratch_{name}", shape, _mybir.dt.float32).ap()
    program(nc, ins, dram, batch)
    r = _run(nc, [arrays], core_ids=[0])
    return r.results[0]["out_0_dram"]
```
